# Optimizing a Trainium2 kernel written in Bass

```python
import numpy as np
import jax
import jax.numpy as jnp

def _softmax(x, axis=-1):
    return jax.nn.softmax(x, axis=axis)

def _gelu(x):
    return jax.nn.gelu(x, approximate=True)

def _silu(x):
    return jax.nn.silu(x)

def _sigmoid(x):
    return jax.nn.sigmoid(x)

def _layernorm(x, axis=-1, eps=1e-05):
    m = jnp.mean(x, axis=axis, keepdims=True)
    v = jnp.var(x, axis=axis, keepdims=True)
    return (x - m) / jnp.sqrt(v + eps)

def _scatter_add(tgt, idx, src, axis=0):
    return tgt.at[idx].add(src)

def _segment_sum(src, seg, n):
    return jax.ops.segment_sum(src, seg, n)
kernel_name = 'mk_decoder_postln_d2_seqx_r8_7f5d3c'

def setup_inputs(seed: int=0):
    np.random.seed(seed)
    _w = jnp.asarray

    def _rec_inputs():
        import jax
        import jax.numpy as jnp
        _rk = jax.random.key(seed)
        x = -0.0003929 + 0.9999 * jax.random.normal(jax.random.fold_in(_rk, 1), (32, 64, 512), jnp.float32)
        _lenS = 64 - jax.random.randint(jax.random.fold_in(_rk, 7), (32,), 0, max(1, 64 // 4) + 1, jnp.int32)
        _lenS2 = 64 - jax.random.randint(jax.random.fold_in(_rk, 8), (32,), 0, max(1, 64 // 4) + 1, jnp.int32)
        _ctx_4096P = jax.random.normal(jax.random.fold_in(_rk, 11), (32, 16, 512), jnp.float32)
        _ctx_4096c = jax.random.dirichlet(jax.random.fold_in(_rk, 511), 0.3 * jnp.ones((16,), jnp.float32), (32, 64))
        _ctx_4096t = jnp.einsum('bsk,bkd->bsd', _ctx_4096c, _ctx_4096P)
        _ctx_4096t = _ctx_4096t * jax.lax.rsqrt(jnp.mean(jnp.square(_ctx_4096t)) + 1e-12) * 0.953939
        ctx_4096 = 2.81802e-05 + 1.00001 * (_ctx_4096t + 0.3 * jax.random.normal(jax.random.fold_in(_rk, 611), (32, 64, 512), jnp.float32))
        pos_BxS2 = jnp.broadcast_to(jnp.arange(64, dtype=jnp.int32), (32, 64))
        _validS = jnp.arange(64)[None, :] < _lenS[:, None]
        _validS2 = jnp.arange(64)[None, :] < _lenS2[:, None]
        _causal = jnp.tril(jnp.ones((64, 64), dtype=bool))
        mask_BxSxS2_ik0 = jnp.where(jnp.broadcast_to(_validS2[:, None, :], (32, 64, 64)), 0, 1).astype(jnp.int32)
        return (x, ctx_4096, pos_BxS2, mask_BxSxS2_ik0)
    x, ctx_4096, pos_BxS2, mask_BxSxS2_ik0 = _rec_inputs()

    def _L0_attn_setup():
        import jax, jax.numpy as jnp
        import numpy as np
        H = 32
        HKV = 8
        D = 512
        HD = D // H
        S = 128
        MASK_OUT = 0.9
        MIN_REMAIN = 128
        THETA = 10000.0

        def rope_tables(seq_len, hd):
            inv_freq = 1.0 / THETA ** (jnp.arange(0, hd, 2, dtype=jnp.float32) / hd)
            t = jnp.arange(seq_len, dtype=jnp.float32)
            freqs = jnp.outer(t, inv_freq)
            emb = jnp.concatenate([freqs, freqs], axis=-1)
            return (jnp.cos(emb), jnp.sin(emb))

        def rotate_half(x):
            x1, x2 = jnp.split(x, 2, axis=-1)
            return jnp.concatenate([-x2, x1], axis=-1)

        def apply_rope(x, cos, sin):
            return x * cos + rotate_half(x) * sin
        key = jax.random.key(seed)
        k0, k1, k2, k3, k4 = jax.random.split(key, 5)
        hidden_states = jax.random.normal(k0, (1, S, D), jnp.float32)
        Wq = jax.random.normal(k1, (D, D), jnp.float32) * 0.02
        Wk = jax.random.normal(k2, (HKV * HD, D), jnp.float32) * 0.02
        Wv = jax.random.normal(k3, (HKV * HD, D), jnp.float32) * 0.02
        Wo = jax.random.normal(k4, (D, D), jnp.float32) * 0.02
        return {'hidden_states': hidden_states, 'Wq': Wq, 'Wk': Wk, 'Wv': Wv, 'Wo': Wo}
    _L0_attn_all = _L0_attn_setup()
    _L0_attn_in = {k: v for k, v in _L0_attn_all.items() if k in ('Wq', 'Wk', 'Wv', 'Wo')}
    del _L0_attn_all

    def _L0_xattn_setup():
        import jax, jax.numpy as jnp
        import numpy as np
        B, S, E = (2, 256, 512)
        H, KVH, D = (32, 8, 128)
        GROUPS = H // KVH
        MAX_POS = 512
        ROPE_THETA = 10000.0

        def _rope_tables(max_pos, dim, theta):
            inv_freq = 1.0 / theta ** (jnp.arange(0, dim, 2, dtype=jnp.float32) / dim)
            t = jnp.arange(max_pos, dtype=jnp.float32)
            freqs = jnp.einsum('i,j->ij', t, inv_freq)
            emb = jnp.concatenate([freqs, freqs], axis=-1)
            return (jnp.cos(emb), jnp.sin(emb))

        def _rotate_half(x):
            x1, x2 = (x[..., :x.shape[-1] // 2], x[..., x.shape[-1] // 2:])
            return jnp.concatenate([-x2, x1], axis=-1)
        key = jax.random.key(seed)
        ks = jax.random.split(key, 8)
        scale_w = 1.0 / np.sqrt(E)
        query = jax.random.normal(ks[0], (B, S, E), dtype=jnp.float32)
        k_in = jax.random.normal(ks[1], (B, S, E), dtype=jnp.float32)
        v_in = jax.random.normal(ks[2], (B, S, E), dtype=jnp.float32)
        position_ids = jnp.broadcast_to(jnp.arange(S, dtype=jnp.int64), (B, S))
        src_mask = jnp.tril(jnp.ones((S, S), dtype=jnp.int32))
        src_mask = jnp.broadcast_to(src_mask, (B, S, S))
        Wq = jax.random.normal(ks[3], (E, H * D), dtype=jnp.float32) * scale_w
        Wk = jax.random.normal(ks[4], (E, KVH * D), dtype=jnp.float32) * scale_w
        Wv = jax.random.normal(ks[5], (E, KVH * D), dtype=jnp.float32) * scale_w
        Wo = jax.random.normal(ks[6], (H * D, E), dtype=jnp.float32) * scale_w
        return {'query': query, 'key': k_in, 'value': v_in, 'position_ids': position_ids, 'src_mask': src_mask, 'Wq': Wq, 'Wk': Wk, 'Wv': Wv, 'Wo': Wo}
    _L0_xattn_all = _L0_xattn_setup()
    _L0_xattn_in = {k: v for k, v in _L0_xattn_all.items() if k in ('Wq', 'Wk', 'Wv', 'Wo')}
    del _L0_xattn_all

    def _L0_ffn_setup():
        import jax, jax.numpy as jnp
        import numpy as np
        DIM = 512
        INTER = 1792
        SPARSITY = 32
        RANK = 16
        key = jax.random.key(seed)
        ks = jax.random.split(key, 5)
        B, T = (32, 1)
        x = jax.random.normal(ks[0], (B, T, DIM), dtype=jnp.float32)
        c1_w = jax.random.normal(ks[1], (RANK, DIM), dtype=jnp.float32) * (1.0 / np.sqrt(DIM))
        c2_w = jax.random.normal(ks[2], (INTER, RANK), dtype=jnp.float32) * (1.0 / np.sqrt(RANK))
        w1 = jax.random.normal(ks[3], (INTER, DIM), dtype=jnp.float32) * (1.0 / np.sqrt(DIM))
        w2t = jax.random.normal(ks[4], (INTER, DIM), dtype=jnp.float32) * (1.0 / np.sqrt(INTER))
        return {'x': x, 'c1_w': c1_w, 'c2_w': c2_w, 'w1': w1, 'w2t': w2t}
    _L0_ffn_all = _L0_ffn_setup()
    _L0_ffn_in = {k: v for k, v in _L0_ffn_all.items() if k in ('c1_w', 'c2_w', 'w1', 'w2t')}
    del _L0_ffn_all

    def _L1_attn_setup():
        import jax, jax.numpy as jnp
        import numpy as np
        DIM = 512
        NUM_HEAD = 32
        NUM_KV_HEAD = 8
        ROPE_THETA = 10000.0
        B, T = (2, 256)

        def apply_rope(x, start_pos=0, theta=ROPE_THETA):
            d = x.shape[-1]
            half = d // 2
            inv_freq = 1.0 / theta ** (jnp.arange(0, half, dtype=jnp.float32) / half)
            pos = jnp.arange(x.shape[1], dtype=jnp.float32) + start_pos
            ang = pos[:, None] * inv_freq[None, :]
            cos = jnp.cos(ang)[None, :, None, :]
            sin = jnp.sin(ang)[None, :, None, :]
            x1, x2 = (x[..., :half], x[..., half:])
            return jnp.concatenate([x1 * cos - x2 * sin, x1 * sin + x2 * cos], axis=-1)
        key = jax.random.key(seed)
        ks = jax.random.split(key, 5)
        scale = 0.02
        X = jax.random.normal(ks[0], (B, T, DIM), dtype=jnp.float32)
        Wq = jax.random.normal(ks[1], (DIM, DIM), dtype=jnp.float32) * scale
        Wk = jax.random.normal(ks[2], (DIM, DIM // NUM_HEAD * NUM_KV_HEAD), dtype=jnp.float32) * scale
        Wv = jax.random.normal(ks[3], (DIM, DIM // NUM_HEAD * NUM_KV_HEAD), dtype=jnp.float32) * scale
        Wo = jax.random.normal(ks[4], (DIM, DIM), dtype=jnp.float32) * scale
        return {'X': X, 'Wq': Wq, 'Wk': Wk, 'Wv': Wv, 'Wo': Wo}
    _L1_attn_all = _L1_attn_setup()
    _L1_attn_in = {k: v for k, v in _L1_attn_all.items() if k in ('Wq', 'Wk', 'Wv', 'Wo')}
    del _L1_attn_all

    def _L1_xattn_setup():
        import jax, jax.numpy as jnp
        import numpy as np
        B, Q, D = (8, 64, 512)
        CTX = 512
        H, KV, HD = (16, 4, 96)
        G = H // KV
        key = jax.random.key(seed)
        ks = jax.random.split(key, 6)
        s = 0.02
        return {'latents': jax.random.normal(ks[0], (B, Q, D), jnp.float32), 'context': jax.random.normal(ks[1], (B, CTX, D), jnp.float32), 'Wq': jax.random.normal(ks[2], (H * HD, D), jnp.float32) * s, 'Wk': jax.random.normal(ks[3], (KV * HD, D), jnp.float32) * s, 'Wv': jax.random.normal(ks[4], (KV * HD, D), jnp.float32) * s, 'Wo': jax.random.normal(ks[5], (D, H * HD), jnp.float32) * s}
    _L1_xattn_all = _L1_xattn_setup()
    _L1_xattn_in = {k: v for k, v in _L1_xattn_all.items() if k in ('Wq', 'Wk', 'Wv', 'Wo')}
    del _L1_xattn_all

    def _L1_ffn_setup():
        import jax, jax.numpy as jnp
        import numpy as np
        BLOCK = 64
        NF4_CODE = jnp.array([-1.0, -0.6961928009986877, -0.5250730514526367, -0.39491748809814453, -0.28444138169288635, -0.18477343022823334, -0.09105003625154495, 0.0, 0.07958029955625534, 0.16093020141124725, 0.24611230194568634, 0.33791524171829224, 0.44070982933044434, 0.5626170039176941, 0.7229568362236023, 1.0], dtype=jnp.float32)

        def dequant_nf4(q, absmax, shape):
            w = NF4_CODE[q.reshape(-1)]
            w = w.reshape(-1, BLOCK) * absmax[:, None]
            return w.reshape(shape)
        key = jax.random.key(seed)
        ks = jax.random.split(key, 7)
        HD, M = (512, 1792)
        nblk = HD * M // BLOCK
        x = jax.random.normal(ks[0], (2, 256, HD), dtype=jnp.float32)
        gate_q = jax.random.randint(ks[1], (M, HD), 0, 16, dtype=jnp.int32)
        up_q = jax.random.randint(ks[2], (M, HD), 0, 16, dtype=jnp.int32)
        down_q = jax.random.randint(ks[3], (HD, M), 0, 16, dtype=jnp.int32)
        gate_absmax = jax.random.uniform(ks[4], (nblk,), dtype=jnp.float32) * 0.05
        up_absmax = jax.random.uniform(ks[5], (nblk,), dtype=jnp.float32) * 0.05
        down_absmax = jax.random.uniform(ks[6], (nblk,), dtype=jnp.float32) * 0.05
        return {'x': x, 'gate_q': gate_q, 'gate_absmax': gate_absmax, 'up_q': up_q, 'up_absmax': up_absmax, 'down_q': down_q, 'down_absmax': down_absmax}
    _L1_ffn_all = _L1_ffn_setup()
    _L1_ffn_in = {k: v for k, v in _L1_ffn_all.items() if k in ('gate_q', 'gate_absmax', 'up_q', 'up_absmax', 'down_q', 'down_absmax')}
    del _L1_ffn_all
    return {'x': x, 'ctx_4096': ctx_4096, 'pos_BxS2': pos_BxS2, 'mask_BxSxS2_ik0': mask_BxSxS2_ik0, 'L0_attn_Wq': _L0_attn_in['Wq'], 'L0_attn_Wk': _L0_attn_in['Wk'], 'L0_attn_Wv': _L0_attn_in['Wv'], 'L0_attn_Wo': _L0_attn_in['Wo'], 'L0_xattn_Wq': _L0_xattn_in['Wq'], 'L0_xattn_Wk': _L0_xattn_in['Wk'], 'L0_xattn_Wv': _L0_xattn_in['Wv'], 'L0_xattn_Wo': _L0_xattn_in['Wo'], 'L0_ffn_c1_w': _L0_ffn_in['c1_w'], 'L0_ffn_c2_w': _L0_ffn_in['c2_w'], 'L0_ffn_w1': _L0_ffn_in['w1'], 'L0_ffn_w2t': _L0_ffn_in['w2t'], 'L1_attn_Wq': _L1_attn_in['Wq'], 'L1_attn_Wk': _L1_attn_in['Wk'], 'L1_attn_Wv': _L1_attn_in['Wv'], 'L1_attn_Wo': _L1_attn_in['Wo'], 'L1_xattn_Wq': _L1_xattn_in['Wq'], 'L1_xattn_Wk': _L1_xattn_in['Wk'], 'L1_xattn_Wv': _L1_xattn_in['Wv'], 'L1_xattn_Wo': _L1_xattn_in['Wo'], 'L1_ffn_gate_q': _L1_ffn_in['gate_q'], 'L1_ffn_gate_absmax': _L1_ffn_in['gate_absmax'], 'L1_ffn_up_q': _L1_ffn_in['up_q'], 'L1_ffn_up_absmax': _L1_ffn_in['up_absmax'], 'L1_ffn_down_q': _L1_ffn_in['down_q'], 'L1_ffn_down_absmax': _L1_ffn_in['down_absmax']}

def reference(x, ctx_4096, pos_BxS2, mask_BxSxS2_ik0, L0_attn_Wq, L0_attn_Wk, L0_attn_Wv, L0_attn_Wo, L0_xattn_Wq, L0_xattn_Wk, L0_xattn_Wv, L0_xattn_Wo, L0_ffn_c1_w, L0_ffn_c2_w, L0_ffn_w1, L0_ffn_w2t, L1_attn_Wq, L1_attn_Wk, L1_attn_Wv, L1_attn_Wo, L1_xattn_Wq, L1_xattn_Wk, L1_xattn_Wv, L1_xattn_Wo, L1_ffn_gate_q, L1_ffn_gate_absmax, L1_ffn_up_q, L1_ffn_up_absmax, L1_ffn_down_q, L1_ffn_down_absmax):
    import jax
    import jax.numpy as jnp

    def _L0_attn_ref(hidden_states, Wq, Wk, Wv, Wo):
        import jax, jax.numpy as jnp
        import numpy as np
        H = 32
        HKV = 8
        D = 512
        HD = D // H
        S = 128
        MASK_OUT = 0.9
        MIN_REMAIN = 128
        THETA = 10000.0

        def rope_tables(seq_len, hd):
            inv_freq = 1.0 / THETA ** (jnp.arange(0, hd, 2, dtype=jnp.float32) / hd)
            t = jnp.arange(seq_len, dtype=jnp.float32)
            freqs = jnp.outer(t, inv_freq)
            emb = jnp.concatenate([freqs, freqs], axis=-1)
            return (jnp.cos(emb), jnp.sin(emb))

        def rotate_half(x):
            x1, x2 = jnp.split(x, 2, axis=-1)
            return jnp.concatenate([-x2, x1], axis=-1)

        def apply_rope(x, cos, sin):
            return x * cos + rotate_half(x) * sin
        B, Sq, Dm = hidden_states.shape
        dtype = hidden_states.dtype
        neg = jnp.finfo(dtype).min
        q = (hidden_states @ Wq.T).reshape(B, Sq, H, HD).transpose(0, 2, 1, 3)
        k = (hidden_states @ Wk.T).reshape(B, Sq, HKV, HD).transpose(0, 2, 1, 3)
        v = (hidden_states @ Wv.T).reshape(B, Sq, HKV, HD).transpose(0, 2, 1, 3)
        rep = H // HKV
        k = jnp.repeat(k, rep, axis=1)
        v = jnp.repeat(v, rep, axis=1)
        cos, sin = rope_tables(Sq, HD)
        qr = apply_rope(q, cos, sin)
        kr = apply_rope(k, cos, sin)
        draft = jnp.einsum('bhqd,bhkd->bhqk', qr, kr)
        qi = jnp.arange(Sq)
        ki = jnp.arange(Sq)
        causal_future = qi[:, None] < ki[None, :]
        draft = draft + jnp.where(causal_future, neg, jnp.asarray(0.0, dtype))
        num_remain = max(min(Sq, MIN_REMAIN), Sq - int(Sq * MASK_OUT))
        _, draft_indices = jax.lax.top_k(draft, num_remain)
        mask = jnp.full((B, H, Sq, Sq), neg, dtype)
        b_idx = jnp.arange(B)[:, None, None, None]
        h_idx = jnp.arange(H)[None, :, None, None]
        s_idx = jnp.arange(Sq)[None, None, :, None]
        mask = mask.at[b_idx, h_idx, s_idx, draft_indices].set(0.0)
        mask = jnp.where(causal_future[None, None, :, :], neg, mask)
        scores = jnp.einsum('bhqd,bhkd->bhqk', qr, kr) / np.sqrt(HD).astype(np.float32) + mask
        attn = jax.nn.softmax(scores, axis=-1)
        out = jnp.einsum('bhqk,bhkd->bhqd', attn, v)
        out = out.transpose(0, 2, 1, 3).reshape(B, Sq, Dm)
        return out @ Wo.T

    def _L0_xattn_ref(query, key, value, position_ids, src_mask, Wq, Wk, Wv, Wo):
        import jax, jax.numpy as jnp
        import numpy as np
        B, S, E = (2, 256, 512)
        H, KVH, D = (32, 8, 128)
        GROUPS = H // KVH
        MAX_POS = 512
        ROPE_THETA = 10000.0

        def _rope_tables(max_pos, dim, theta):
            inv_freq = 1.0 / theta ** (jnp.arange(0, dim, 2, dtype=jnp.float32) / dim)
            t = jnp.arange(max_pos, dtype=jnp.float32)
            freqs = jnp.einsum('i,j->ij', t, inv_freq)
            emb = jnp.concatenate([freqs, freqs], axis=-1)
            return (jnp.cos(emb), jnp.sin(emb))

        def _rotate_half(x):
            x1, x2 = (x[..., :x.shape[-1] // 2], x[..., x.shape[-1] // 2:])
            return jnp.concatenate([-x2, x1], axis=-1)
        nb, q_len, _ = query.shape
        q = (query @ Wq).reshape(nb, q_len, H, D).transpose(0, 2, 1, 3)
        k = (key @ Wk).reshape(nb, q_len, KVH, D).transpose(0, 2, 1, 3)
        v = (value @ Wv).reshape(nb, q_len, KVH, D).transpose(0, 2, 1, 3)
        cos_t, sin_t = _rope_tables(MAX_POS, D, ROPE_THETA)
        cos = cos_t[position_ids][:, None]
        sin = sin_t[position_ids][:, None]
        q = q * cos + _rotate_half(q) * sin
        k = k * cos + _rotate_half(k) * sin
        k = jnp.repeat(k, GROUPS, axis=1)
        v = jnp.repeat(v, GROUPS, axis=1)
        scores = jnp.einsum('bhqd,bhkd->bhqk', q, k) / jnp.sqrt(jnp.float32(D))
        mask = src_mask[:, None]
        scores = jnp.where(mask == 0, jnp.float32(-1000000000.0), scores)
        attn = jax.nn.softmax(scores, axis=-1)
        x = jnp.einsum('bhqk,bhkd->bhqd', attn, v)
        x = x.transpose(0, 2, 1, 3).reshape(nb, q_len, H * D)
        return x @ Wo

    def _L0_ffn_ref(x, c1_w, c2_w, w1, w2t):
        import jax, jax.numpy as jnp
        import numpy as np
        DIM = 512
        INTER = 1792
        SPARSITY = 32
        RANK = 16
        B, T, M = x.shape
        xf = x.reshape(B * T, M)
        inter = xf @ c1_w.T @ c2_w.T
        n_blocks = INTER // SPARSITY
        blk = inter.reshape(B * T, n_blocks, SPARSITY)
        idx = jnp.argmax(blk, axis=-1) + jnp.arange(0, INTER, SPARSITY)
        w1_g = w1[idx]
        w2_g = w2t[idx]
        h = jax.nn.relu(jnp.einsum('bkm,bm->bk', w1_g, xf))
        out = jnp.einsum('bk,bkm->bm', h, w2_g)
        return out.reshape(B, T, M)

    def _L1_attn_ref(X, Wq, Wk, Wv, Wo):
        import jax, jax.numpy as jnp
        import numpy as np
        DIM = 512
        NUM_HEAD = 32
        NUM_KV_HEAD = 8
        ROPE_THETA = 10000.0
        B, T = (2, 256)

        def apply_rope(x, start_pos=0, theta=ROPE_THETA):
            d = x.shape[-1]
            half = d // 2
            inv_freq = 1.0 / theta ** (jnp.arange(0, half, dtype=jnp.float32) / half)
            pos = jnp.arange(x.shape[1], dtype=jnp.float32) + start_pos
            ang = pos[:, None] * inv_freq[None, :]
            cos = jnp.cos(ang)[None, :, None, :]
            sin = jnp.sin(ang)[None, :, None, :]
            x1, x2 = (x[..., :half], x[..., half:])
            return jnp.concatenate([x1 * cos - x2 * sin, x1 * sin + x2 * cos], axis=-1)
        Bs, Ts, C = X.shape
        H, Hkv = (NUM_HEAD, NUM_KV_HEAD)
        dh = C // H
        G = H // Hkv
        Q = apply_rope((X @ Wq).reshape(Bs, Ts, H, dh))
        K = apply_rope((X @ Wk).reshape(Bs, Ts, Hkv, dh))
        V = (X @ Wv).reshape(Bs, Ts, Hkv, dh)
        Qh = Q.transpose(0, 2, 1, 3).reshape(Bs, Hkv, G, Ts, dh)
        Kh = K.transpose(0, 2, 1, 3)
        Vh = V.transpose(0, 2, 1, 3)
        scores = jnp.einsum('bkgtd,bksd->bkgts', Qh, Kh) / jnp.sqrt(jnp.float32(dh))
        causal = jnp.tril(jnp.ones((Ts, Ts), dtype=bool))
        scores = jnp.where(causal[None, None, None], scores, -jnp.inf)
        attn = jax.nn.softmax(scores, axis=-1)
        out = jnp.einsum('bkgts,bksd->bkgtd', attn, Vh)
        out = out.reshape(Bs, H, Ts, dh).transpose(0, 2, 1, 3).reshape(Bs, Ts, C)
        return out @ Wo

    def _L1_xattn_ref(latents, context, Wq, Wk, Wv, Wo):
        import jax, jax.numpy as jnp
        import numpy as np
        B, Q, D = (8, 64, 512)
        CTX = 512
        H, KV, HD = (16, 4, 96)
        G = H // KV
        b, q_len, _ = latents.shape
        hidden = jnp.concatenate([context, latents], axis=1)
        s_len = hidden.shape[1]
        q = (latents @ Wq.T).reshape(b, q_len, H, HD)
        k = (hidden @ Wk.T).reshape(b, s_len, KV, HD)
        v = (hidden @ Wv.T).reshape(b, s_len, KV, HD)
        q = q.transpose(0, 2, 1, 3).reshape(b, KV, G, q_len, HD)
        k = k.transpose(0, 2, 1, 3)
        v = v.transpose(0, 2, 1, 3)
        scale = 1.0 / jnp.sqrt(jnp.asarray(HD, q.dtype))
        scores = jnp.einsum('bkgqd,bksd->bkgqs', q, k) * scale
        attn = jax.nn.softmax(scores.astype(jnp.float32), axis=-1).astype(q.dtype)
        out = jnp.einsum('bkgqs,bksd->bkgqd', attn, v)
        out = out.reshape(b, H, q_len, HD).transpose(0, 2, 1, 3).reshape(b, q_len, H * HD)
        return out @ Wo.T

    def _L1_ffn_ref(x, gate_q, gate_absmax, up_q, up_absmax, down_q, down_absmax):
        import jax, jax.numpy as jnp
        import numpy as np
        BLOCK = 64
        NF4_CODE = jnp.array([-1.0, -0.6961928009986877, -0.5250730514526367, -0.39491748809814453, -0.28444138169288635, -0.18477343022823334, -0.09105003625154495, 0.0, 0.07958029955625534, 0.16093020141124725, 0.24611230194568634, 0.33791524171829224, 0.44070982933044434, 0.5626170039176941, 0.7229568362236023, 1.0], dtype=jnp.float32)

        def dequant_nf4(q, absmax, shape):
            w = NF4_CODE[q.reshape(-1)]
            w = w.reshape(-1, BLOCK) * absmax[:, None]
            return w.reshape(shape)
        HD = x.shape[-1]
        M = gate_q.shape[0]
        Wg = dequant_nf4(gate_q, gate_absmax, (M, HD))
        Wu = dequant_nf4(up_q, up_absmax, (M, HD))
        Wd = dequant_nf4(down_q, down_absmax, (HD, M))
        g = jnp.einsum('bsh,mh->bsm', x, Wg)
        u = jnp.einsum('bsh,mh->bsm', x, Wu)
        h = jax.nn.silu(g) * u
        return jnp.einsum('bsm,hm->bsh', h, Wd)
    x = _layernorm(x + _L0_attn_ref(x, L0_attn_Wq, L0_attn_Wk, L0_attn_Wv, L0_attn_Wo), axis=-1)
    x = _layernorm(x + _L0_xattn_ref(x, ctx_4096, ctx_4096, pos_BxS2, mask_BxSxS2_ik0, L0_xattn_Wq, L0_xattn_Wk, L0_xattn_Wv, L0_xattn_Wo), axis=-1)
    x = _layernorm(x + _L0_ffn_ref(x, L0_ffn_c1_w, L0_ffn_c2_w, L0_ffn_w1, L0_ffn_w2t), axis=-1)
    x = _layernorm(x + _L1_attn_ref(x, L1_attn_Wq, L1_attn_Wk, L1_attn_Wv, L1_attn_Wo), axis=-1)
    x = _layernorm(x + _L1_xattn_ref(x, ctx_4096, L1_xattn_Wq, L1_xattn_Wk, L1_xattn_Wv, L1_xattn_Wo), axis=-1)
    x = _layernorm(x + _L1_ffn_ref(x, L1_ffn_gate_q, L1_ffn_gate_absmax, L1_ffn_up_q, L1_ffn_up_absmax, L1_ffn_down_q, L1_ffn_down_absmax), axis=-1)
    return x

_drawn_inputs = setup_inputs


def setup_inputs(seed=0):
    import zlib

    import numpy as np

    out = dict(_drawn_inputs(seed))
    spreads = {}
    factors = {'L0_attn_Wq': 4.414,
     'L0_attn_Wk': 4.143,
     'L1_attn_Wq': 8.0,
     'L1_attn_Wk': 8.0,
     'L1_xattn_Wq': 3.134,
     'L1_xattn_Wk': 3.071,
     'L1_ffn_gate_absmax': 2.982,
     'L1_ffn_up_absmax': 3.035,
     'L1_ffn_down_absmax': 3.032}
    for name, (base, spread) in spreads.items():
        noise = np.random.default_rng([zlib.crc32(name.encode()), seed]).standard_normal(out[name].shape)
        drawn = base * np.exp(spread * noise) if base else spread * noise
        out[name] = jnp.asarray(drawn.astype(out[name].dtype))
    for name, factor in factors.items():
        out[name] = (out[name] * factor).astype(out[name].dtype)
    return out
```

```python
from contextlib import ExitStack

import concourse.bass as bass
from concourse import mybir
import numpy as np

ALU = mybir.AluOpType
ACT = mybir.ActivationFunctionType
AX = mybir.AxisListType
F32 = mybir.dt.float32
BF16 = mybir.dt.bfloat16
I32 = mybir.dt.int32
U16 = mybir.dt.uint16

P = 128
BATCH, SEQ, DIM = 32, 64, 512
TOK = BATCH * SEQ
GROUPS = 4
GT = TOK // GROUPS
GB = BATCH // GROUPS
TILES = GT // P
KC = DIM // P
INTER = 1792
ROW = 256
FSETS = INTER // ROW
BLK = 32
RANK = 16
POSITIONS = 512
EPS = 1e-5
CODE = np.array([-1.0, -0.6961928009986877, -0.5250730514526367, -0.39491748809814453,
                 -0.28444138169288635, -0.18477343022823334, -0.09105003625154495, 0.0,
                 0.07958029955625534, 0.16093020141124725, 0.24611230194568634, 0.33791524171829224,
                 0.44070982933044434, 0.5626170039176941, 0.7229568362236023, 1.0], np.float32)
FUTURE = -3.0e38
MASKED = -1.0e9 * float(np.sqrt(128.0))
TIE = 64.0

HD16, CROSS0, CROSS1 = "heads of 16", "cross-attention 0", "cross-attention 1"
SCALE = {HD16: 0.25, CROSS0: 128.0 ** -0.5, CROSS1: 96.0 ** -0.5}
UNITS = {HD16: GB, CROSS0: 1, CROSS1: 2}
OUT_USES = {HD16: 1, CROSS0: 4, CROSS1: 2}
STAGES = [(0, HD16, 1), (1, CROSS0, 8), (2, "ffn0", FSETS), (3, HD16, 1), (4, CROSS1, 4), (5, "ffn1", FSETS)]
CODES_USED = [k for k in range(16) if CODE[k] != 0.0]
PIECES = 3 * (len(CODES_USED) + 1)


class Use:

    def __init__(self, n, act, dve):
        self.n, self.act, self.dve = n, act, dve


class Task:

    def __init__(self, stage, kind, group, sub, wset, last_set, first):
        self.stage, self.kind, self.group, self.sub, self.wset = stage, kind, group, sub, wset
        self.last_set, self.first = last_set, first


class Unit:

    def __init__(self, task, i, n, last):
        self.task, self.i, self.n, self.first, self.last = task, i, n, i == 0, last


class Step:

    def __init__(self, kind, plan, task=None, unit=None, group=None, n=None, stage=None):
        self.kind, self.task, self.unit, self.group, self.n, self.stage = kind, task, unit, group, n, stage
        self.pp_before, self.sc_before = plan.count("pp"), plan.count("sc")
        self.tr_before, self.ou_before = plan.count("tr"), plan.count("ou")
        self.kbd_before = plan.kbds
        self.added = plan.read["ou", "dve"]
        self.final = stage == STAGES[-1][0]
        self.pieces = (0, 0)


class Plan:

    def __init__(self):
        self.rings = {r: [] for r in ("pp", "sc", "tr", "ou")}
        self.read = {(r, e): 0 for r in self.rings for e in ("act", "dve")}
        self.steps = []
        self.units = self.tasks = self.ropes = self.kbds = self.norms = self.ffns = self.g1s = 0
        self.set_done = {}
        self.turned = {}
        self.hd_units = []
        self.build()
        self.place_dequantising()

    def use(self, ring, readers, count):
        out = []
        for _ in range(count):
            for e in readers:
                self.read[ring, e] += 1
            u = Use(len(self.rings[ring]), self.read[ring, "act"] if "act" in readers else None,
                    self.read[ring, "dve"] if "dve" in readers else None)
            self.rings[ring].append(u)
            out.append(u)
        return out

    def alternate(self, ring, count):
        return [self.use(ring, (("act",), ("dve",))[i % 2], 1)[0] for i in range(count)]

    def count(self, ring):
        return len(self.rings[ring])

    def add(self, kind, **fields):
        s = Step(kind, self, **fields)
        self.steps.append(s)
        return s

    def project(self, task):
        s = self.add("A", task=task)
        if task.kind == CROSS1:
            s.q, s.k, s.v = self.alternate("pp", 4), self.alternate("pp", 2), self.alternate("pp", 2)
        else:
            s.q, s.k = self.use("pp", ("act", "dve"), 4), self.use("pp", ("act", "dve"), 1)
            s.v = self.use("pp", ("act", "dve") if task.kind == HD16 else ("act",), 1)
        s.rope = self.ropes
        if task.kind != CROSS1:
            self.ropes += 5
        task.a = s
        task.rope_done = self.ropes

    def scores(self, unit):
        s = self.add("B", unit=unit)
        if unit.task.kind == HD16:
            unit.kbd = self.kbds
            self.kbds += 1
            self.hd_units.append(unit)
            unit.task.last_kbd = unit.kbd
        s.sc = self.use("sc", ("dve",), 2)
        unit.b = s

    def turn(self, unit):
        s = self.add("T", unit=unit)
        s.tr = self.use("tr", ("act",), 2)
        unit.t = s

    def values(self, unit):
        s = self.add("C", unit=unit)
        s.ou = self.use("ou", ("act",), OUT_USES[unit.task.kind])
        unit.c = s
        if unit.last:
            unit.task.c_done = self.count("ou")

    def output(self, task):
        s = self.add("D", task=task)
        s.ou = self.use("ou", ("dve",), TILES)
        task.d = s
        self.set_done[task.wset] = self.count("ou")
        self.after(task)

    def after(self, task):
        if task.last_set:
            self.pending.append(self.add("LN", group=task.group, n=self.norms, stage=task.stage))
            self.norms += 1

    def turn_norms(self, keep=0):
        while len(self.pending) > keep:
            ln = self.pending.pop(0)
            if not ln.final:
                s = self.add("LNT", group=ln.group, n=ln.n, stage=ln.stage)
                s.tr = self.use("tr", ("act",), TILES)
                self.turned[ln.n] = s

    def build(self):
        self.pending = []
        for t in range(GROUPS):
            s = self.add("POS", group=t)
            s.pp = self.alternate("pp", 2)
        wset = 0
        self.by_unit = []
        waiting = []
        owed = []

        def finish_one():
            v = waiting.pop(0)
            self.turn(v)
            if owed:
                self.output(owed.pop(0))
            self.values(v)
            if v.last:
                owed.append(v.task)

        for stage, kind, sets in STAGES:
            tasks = []
            for s in range(sets):
                for t in range(GROUPS):
                    tasks.append(Task(stage=stage, kind=kind, group=t, sub=s, wset=wset + s,
                                      last_set=s == sets - 1, first=(s == 0 and t == 0)))
            wset += sets
            if kind in (HD16, CROSS0, CROSS1):
                if kind == CROSS0:
                    while waiting:
                        finish_one()
                    self.add("MASK")
                for task in tasks:
                    task.n = self.tasks
                    self.tasks += 1
                    while self.pending and self.pending[0].n <= GROUPS * (stage - 1) + task.group:
                        self.turn_norms(len(self.pending) - 1)
                    for i in range(UNITS[kind]):
                        u = Unit(task, i, self.units, last=i == UNITS[kind] - 1)
                        self.units += 1
                        self.by_unit.append(u)
                        if i == 0:
                            self.project(task)
                        self.scores(u)
                        if waiting:
                            finish_one()
                        waiting.append(u)
                        self.turn_norms(0 if i == 1 else 1)
                continue
            while waiting:
                finish_one()
            while owed:
                self.output(owed.pop(0))
            self.turn_norms()
            if kind == "ffn0":
                self.add("FC")
                for t in range(GROUPS):
                    s = self.add("Z", group=t)
                    s.pp = self.use("pp", ("act",), 1)

                def f1(task):
                    task.n = self.ffns
                    self.ffns += 1
                    task.f1 = self.add("F1", task=task)
                    task.f1.sc = self.use("sc", ("dve",), 2)
                    task.f1.pp = self.alternate("pp", 2)

                def f2(task):
                    task.f2 = self.add("F2", task=task)
                    task.f2.tr = self.use("tr", ("act",), 2)

                def f3(task):
                    task.f3 = self.add("F3", task=task)
                    task.f3.sc = self.use("sc", ("dve",), 2)

                def f4(task):
                    task.f4 = self.add("F4", task=task)
                    task.f4.ou = self.use("ou", ("dve",), TILES)
                    self.set_done[task.wset] = self.count("ou")
                    self.after(task)

                f1(tasks[0])
                for i, task in enumerate(tasks):
                    if i + 1 < len(tasks):
                        f1(tasks[i + 1])
                    f2(task)
                    if i:
                        f4(tasks[i - 1])
                    f3(task)
                f4(tasks[-1])
            else:
                def g1(task):
                    task.n = self.g1s
                    self.g1s += 1
                    task.g1 = self.add("G1", task=task)
                    task.g1.gate = self.use("pp", ("act",), 2)
                    task.g1.up = self.use("sc", ("dve",), 2)

                def g2(task):
                    task.g2 = self.add("G2", task=task)
                    task.g2.ou = self.use("ou", ("dve",), TILES)
                    self.after(task)

                g1(tasks[0])
                for i, task in enumerate(tasks):
                    if i + 1 < len(tasks):
                        g1(tasks[i + 1])
                    g2(task)

    def place_dequantising(self):
        at = 0
        steps = [s for s in self.steps if s.kind == "B" and s.unit.task.kind == CROSS1][2:]
        for s in steps:
            s.pieces = (at, at + 2)
            at += 2
        for s in self.steps:
            if s.kind == "G2":
                end = min(at + 12, FSETS * PIECES)
                s.pieces = (at, end)
                at = end
        assert at == FSETS * PIECES


def decoder_kernel(nc, x_tok, x_T, ctx_T, pos, mask, hd_w, cross0_w, c1T, c2T, w1T, w2t, cross1_w,
                   gate_q, gate_s, up_q, up_s, down_q, down_s, consts, out):
    plan = Plan()
    steps = plan.steps
    cross_tasks = [s.task for s in steps if s.kind == "A"]
    units = plan.by_unit
    hd_units = plan.hd_units
    first_cross1 = next(u for u in units if u.task.kind == CROSS1)

    with ExitStack() as ctx:
        def sb(name, shape, dt=F32):
            return ctx.enter_context(nc.sbuf_tensor(name, shape, dt))

        def sem(name):
            return ctx.enter_context(nc.semaphore(name))

        X = sb("X", [P, TOK // P, DIM])
        HT = sb("HT", [P, KC, 2 * TOK])
        W = sb("W", [P, 2 * 5120])
        QT = sb("QT", [P, GB, 4, SEQ])
        OT = sb("OT", [P, 4, GT])
        PT = sb("PT", [P, 2, 1024])
        E = sb("E", [P, 4, 512])
        SW = sb("SW", [P, 2, 512])
        KR = sb("KR", [P, 1536])
        VR = sb("VR", [P, 2, 1024])
        AUX = sb("AUX", [P, 4096])
        VB = sb("VB", [P, 2, 512])
        ident = sb("ident", [P, P])
        causal = sb("causal", [P, SEQ])
        rope16 = sb("rope16", [P, 2, SEQ])
        small = sb("small", [P, 152])
        taken = [0]

        def part(*shape):
            n = int(np.prod(shape))
            ap = small[:, taken[0]:taken[0] + n]
            taken[0] += n
            return ap.rearrange("p (a b) -> p a b", a=shape[0]) if len(shape) == 2 else ap

        own_head = part(8)
        masked = part(1)
        mx, sums, rinv = part(4, 8), part(4, 8), part(4, 8)
        stats, meanvar = part(TILES, 6), part(TILES, 2)
        vareps, rstd, minus_half = part(TILES), part(TILES), part(TILES)

        KT = KR[:, 0:512]
        KT1 = KR[:, 0:1024]
        Kbd = KR[:, 512:1536].rearrange("p (r n) -> p r n", r=2)
        amask = KR[:, 512:1536].bitcast(U16)
        mask_raw = PT[:, :, :].rearrange("p a n -> p (a n)").bitcast(I32)
        cosT, sinT = AUX[:, 0:TOK], AUX[:, TOK:2 * TOK]
        posi = W[:, 5120:5120 + 2048].bitcast(I32)
        posf = W[:, 5120:5120 + 2048]
        onehot = W[:, 7168:8192].rearrange("p (r n) -> p r n", r=2)
        ptab = W[:, 8192:9216].rearrange("p (k n) -> p k n", k=4)
        iota = W[:, 9216:9220]
        QTf = QT[:, :, :, :].rearrange("p b a n -> p (b a n)")
        paired = HT[:, :, :].rearrange("p c (b e s) -> p c b e s", e=2, s=SEQ)
        OTf = OT[:, :, :].rearrange("p a n -> p (a n)")
        PTf = PT[:, :, :].rearrange("p a n -> p (a n)")
        Ef = E[:, :, :].rearrange("p a n -> p (a n)")
        SWf = SW[:, :, :].rearrange("p a n -> p (a n)")
        VBf = VB[:, :, :].rearrange("p a n -> p (a n)")
        zT = AUX[0:RANK, 0:TOK]
        chosen = QTf[:, 0:1024].bitcast(BF16).rearrange("p (r i n) -> p r i n", r=2, i=TILES)
        chosenT = QTf[:, 1024:1536].bitcast(BF16).rearrange("p (c n) -> p c n", c=2)
        relu = OTf.rearrange("p (r c n) -> p r c n", r=2, c=2)
        hsel = PTf[:, 0:1024].rearrange("p (c n) -> p c n", c=2)
        blkmax = sums
        ties = Ef[:, 0:64].bitcast(BF16)
        ties_f = PTf[:, 1024:1024 + P]
        ident_b = Ef[:, 64:128].bitcast(BF16)
        c1_sb = Ef[:, 128:192].rearrange("p (c n) -> p c n", c=KC)
        c2_sb = Ef[0:RANK, 192:192 + INTER]
        silu = PTf.rearrange("p (r c n) -> p r c n", r=2, c=2)
        hgate = OTf.rearrange("p (r c n) -> p r c n", r=2, c=2)
        dq = [AUX[:, 0:3072], W[:, 5120:8192]]
        dq_q = SWf.bitcast(I32)
        dq_s = AUX[:, 3072:4096]
        dq_b = VBf[:, 0:512].bitcast(BF16)
        dq_e = VBf[:, 512:1024].bitcast(BF16)

        def x_cols(stage, c, group):
            if stage <= 3:
                return HT[:, c, TOK + group * GT:TOK + (group + 1) * GT]
            return paired[:, c, group * GB:(group + 1) * GB, 1, :]

        def wslot(wset):
            return W[:, 5120 * (wset % 2):5120 * (wset % 2) + 5120]

        def weights(kind, wset):
            w = wslot(wset)
            if kind == CROSS1:
                return (w[:, 0:1536].rearrange("p (c n) -> p c n", c=KC),
                        w[:, 1536:1920].rearrange("p (c n) -> p c n", c=KC),
                        w[:, 1920:2304].rearrange("p (c n) -> p c n", c=KC),
                        w[0:96, 2304:4352].rearrange("p (j n) -> p j n", j=4))
            return (w[:, 0:2048].rearrange("p (c n) -> p c n", c=KC),
                    w[:, 2048:2560].rearrange("p (c n) -> p c n", c=KC),
                    w[:, 2560:3072].rearrange("p (c n) -> p c n", c=KC),
                    w[:, 3072:5120].rearrange("p (j n) -> p j n", j=4))

        def ffn_weights(w):
            return (w[:, 0:1024].rearrange("p (c n) -> p c n", c=KC),
                    w[:, 1024:2048].rearrange("p (c n) -> p c n", c=2))

        def v_buf(task):
            return VR[:, task.n % 2, :]

        banks = {r: [ctx.enter_context(nc.psum_tensor(f"{r}{i}", [P, 512], F32)) for i in range(2)]
                 for r in ("pp", "sc", "tr", "ou")}

        def bank(ring, u):
            return banks[ring][u.n % 2]

        full = {r: sem(f"{r}_full") for r in banks}
        by_act = {r: sem(f"{r}_read_by_act") for r in banks}
        by_dve = {r: sem(f"{r}_read_by_dve") for r in banks}
        s_const = sem("consts_loaded")
        s_pos = sem("positions_loaded")
        s_x = sem("x_loaded")
        s_ht = sem("xT_loaded")
        s_ctx = sem("ctxT_loaded")
        s_paired = [sem(f"paired_context_{g}_loaded") for g in range(GROUPS)]
        s_w = [sem("weights_even_loaded"), sem("weights_odd_loaded")]
        s_mraw = sem("mask_loaded")
        s_fc = sem("ffn0_consts_loaded")
        s_fcb = sem("ffn0_consts_in_bf16")
        s_init = sem("buffers_initialised")
        s_posf = sem("positions_ready")
        s_oh = sem("onehot_ready")
        s_ohused = sem("onehot_used")
        s_amask = sem("mask_ready")
        s_swap = sem("swapped_halves")
        s_swsin = sem("swapped_times_sin")
        s_rope = sem("rope_done")
        s_kbd = sem("kbd_ready")
        s_vbd = sem("vbd_ready")
        s_max = sem("row_max")
        s_pred = sem("mask_applied")
        s_sub = sem("max_subtracted")
        s_exp = sem("exp_done")
        s_sum = sem("row_sum")
        s_rinv = sem("row_sum_inverted")
        s_prob = sem("probs_ready")
        s_stat = sem("tile_stats")
        s_mv = sem("mean_var")
        s_ve = sem("var_plus_eps")
        s_rstd = sem("rstd_ready")
        s_xn = sem("x_normed")
        s_bmax = sem("block_max")
        s_chosen = sem("chosen_ready")
        s_hsel = by_dve["sc"]
        s_dqq = sem("dq_codes_loaded")
        s_dqs = sem("dq_scales_loaded")
        s_dqb = sem("dq_codes_converted")
        s_dqe = sem("dq_equal")
        s_dqa = sem("dq_added")
        s_dqd = sem("dq_matrix_done")
        s_out = sem("out_stored")

        block = ctx.enter_context(nc.Block())

        def set_kind(w):
            for stage, kind, sets in STAGES:
                if w < sets:
                    return stage, kind, w
                w -= sets
            return None

        dma_count = [0, 0]
        loaded = {}
        n_sets = sum(s for _, k, s in STAGES if k != "ffn1")
        for w in range(n_sets):
            _, kind, _ = set_kind(w)
            dma_count[w % 2] += 16 * (2 if kind == "ffn0" else 4)
            loaded[w] = dma_count[w % 2]

        stage3 = [t for t in cross_tasks if t.stage == 3]
        ffn_tasks = [st.task for st in steps if st.kind == "F1"]
        gate_tasks = [st.task for st in steps if st.kind == "G1"]
        cross0_first = next(t.n for t in cross_tasks if t.kind == CROSS0)

        def blocked(ap, n):
            return ap.rearrange("p (g k) -> p g k", g=n)

        def read(eng, ring, *uses):
            for u in uses:
                if u.act is not None:
                    eng.wait_ge(by_act[ring], u.act)
                if u.dve is not None:
                    eng.wait_ge(by_dve[ring], u.dve)

        def before(task):
            return cross_tasks[task.n - 1]

        def values_free(eng, task):
            if task.n >= 2:
                old = cross_tasks[task.n - 2]
                if old.kind == HD16:
                    eng.wait_ge(s_vbd, old.last_kbd + 1)
                else:
                    eng.wait_ge(full["ou"], old.c_done)

        per_matrix = len(CODES_USED) + 1

        @block.sync
        def _(sp):
            for dst, name in ((ident[:, :], "ident"), (causal[:, :], "causal"), (own_head, "own_head"), (iota, "iota")):
                sp.dma_start(dst, consts[name]).then_inc(s_const, 16)
            sp.dma_start(rope16[:, :, :], consts["rope16"]).then_inc(s_const, 16)
            sp.dma_start(ptab, consts["ptab"].rearrange("(k p) n -> p k n", p=P)).then_inc(s_pos, 16)
            sp.dma_start(posi, pos.to_broadcast([P, TOK])).then_inc(s_pos, 16)

            def load_set(w):
                stage, kind, sub = set_kind(w)
                s = s_w[w % 2]
                dst = W[:, 5120 * (w % 2):5120 * (w % 2) + 5120]
                if kind == "ffn0":
                    a, b = ffn_weights(dst)
                    sp.dma_start(a, w1T[:, sub * ROW:(sub + 1) * ROW].rearrange("(c p) n -> p c n", p=P)).then_inc(s, 16)
                    sp.dma_start(b, w2t[sub * ROW:(sub + 1) * ROW, :].rearrange("(c p) n -> p c n", p=P)).then_inc(s, 16)
                    return
                q, k, v, o = weights(kind, w)
                if kind == HD16:
                    dq_, dk, dv, do = hd_w[0 if stage == 0 else 1]
                    width, head = 512, P
                elif kind == CROSS0:
                    dq_, dk, dv, do = cross0_w
                    width, head = 512, P
                else:
                    dq_, dk, dv, do = cross1_w
                    width, head = 384, 96
                sp.dma_start(q, dq_[:, sub * width:(sub + 1) * width].rearrange("(c p) n -> p c n", p=P)).then_inc(s, 16)
                sp.dma_start(k, dk[:, sub * head:(sub + 1) * head].rearrange("(c p) n -> p c n", p=P)).then_inc(s, 16)
                sp.dma_start(v, dv[:, sub * head:(sub + 1) * head].rearrange("(c p) n -> p c n", p=P)).then_inc(s, 16)
                sp.dma_start(o, do[sub * width:(sub + 1) * width, :].rearrange("(j p) n -> p j n", p=head)).then_inc(s, 16)

            def load_codes(m):
                s, which = divmod(m, 3)
                if m:
                    sp.wait_ge(s_dqb, m)
                else:
                    sp.wait_ge(s_rope, plan.ropes)
                    sp.wait_ge(full["ou"], plan.hd_units[-1].task.d.ou[-1].n + 1)
                q = (gate_q, up_q, down_q)[which]
                if which < 2:
                    dst = dq_q.rearrange("p (c n) -> p c n", c=KC)
                    src = q[:, s * ROW:(s + 1) * ROW].rearrange("(c p) n -> p c n", p=P)
                else:
                    dst = dq_q.rearrange("p (c n) -> p c n", c=2)
                    src = q[s * ROW:(s + 1) * ROW, :].rearrange("(c p) n -> p c n", p=P)
                sp.dma_start(dst, src).then_inc(s_dqq, 16)

            def load_scales(m):
                s, which = divmod(m, 3)
                if m:
                    sp.wait_ge(s_dqd, m)
                for half in range(2):
                    if which < 2:
                        sc = (gate_s, up_s)[which].rearrange("(c h) n -> h c n", h=2)[half, :, s * ROW:(s + 1) * ROW]
                        dst = dq_s[64 * half:64 * half + 64, :].rearrange("p (c n) -> p c n", c=KC)
                        shape = [64, KC, ROW]
                    else:
                        sc = down_s[4 * s:4 * s + 4, :].rearrange("(c h) n -> h c n", h=2)[half, :, :]
                        dst = dq_s[64 * half:64 * half + 64, :].rearrange("p (c n) -> p c n", c=2)
                        shape = [64, 2, DIM]
                    sp.dma_start(dst, sc.unsqueeze(0).to_broadcast(shape)).then_inc(s_dqs, 16)

            def load_paired(group):
                for c in range(KC):
                    src = ctx_T[c * P:(c + 1) * P, group * GT:(group + 1) * GT]
                    sp.dma_start(paired[:, c, group * GB:(group + 1) * GB, 0, :],
                                 src.rearrange("p (b s) -> p b s", s=SEQ)).then_inc(s_paired[group], 16)

            load_set(0)
            for c in range(KC):
                sp.dma_start(HT[:, c, TOK:2 * TOK], x_T[c * P:(c + 1) * P, :]).then_inc(s_ht, 16)
            for t in range(GROUPS):
                sp.dma_start(X[:, t * TILES:(t + 1) * TILES, :],
                             x_tok[t * GT:(t + 1) * GT, :].rearrange("(n p) d -> p n d", p=P)).then_inc(s_x, 16)
            for c in range(KC):
                sp.dma_start(HT[:, c, 0:TOK], ctx_T[c * P:(c + 1) * P, :]).then_inc(s_ctx, 16)
            sp.wait_ge(full["pp"], 2 * GROUPS)
            sp.wait_ge(s_oh, 4 * GROUPS)
            load_set(1)
            for st in steps:
                if st.kind == "FC":
                    sp.wait_ge(full["pp"], st.pp_before)
                    load_paired(0)
                    load_paired(1)
                if st.kind == "LN" and st.stage == 3 and st.group in (1, 3):
                    sp.wait_ge(full["pp"], stage3[st.group].a.v[-1].n + 1)
                    load_paired(2 + st.group // 2)
                if st.kind == "MASK":
                    sp.wait_ge(full["ou"], st.ou_before)
                    src = mask.rearrange("b q k -> q b k")
                    raw = mask_raw.rearrange("p (b k) -> p b k", k=SEQ)
                    for half in range(2):
                        sp.dma_start(raw[64 * half:64 * half + 64], src).then_inc(s_mraw, 16)
                if st.kind == "FC":
                    sp.wait_ge(full["tr"], st.tr_before)
                    sp.wait_ge(full["ou"], st.ou_before)
                    sp.dma_start(ties_f, consts["ties"]).then_inc(s_fc, 16)
                    sp.dma_start(c1_sb, c1T.rearrange("(c p) n -> p c n", p=P)).then_inc(s_fc, 16)
                    sp.dma_start(c2_sb, c2T).then_inc(s_fc, 16)
                done = None
                if st.kind in ("D", "F4") and st.task.group == GROUPS - 1:
                    done = st.task.wset
                if done is not None and done + 2 < n_sets:
                    sp.wait_ge(full["ou"], plan.set_done[done])
                    load_set(done + 2)
                for p in range(*st.pieces):
                    m, k = divmod(p, per_matrix)
                    if k == 1 and m + 1 < 3 * FSETS:
                        load_codes(m + 1)
                    if k == per_matrix - 1 and m + 1 < 3 * FSETS:
                        load_scales(m + 1)
                if st.kind == "B" and st.unit is first_cross1:
                    load_codes(0)
                    load_scales(0)
                if st.kind == "LN" and st.final:
                    sp.wait_ge(s_xn, TILES * (st.n + 1))
                    g = st.group
                    sp.dma_start(out[g * GT:(g + 1) * GT, :].rearrange("(n p) d -> p n d", p=P),
                                 X[:, g * TILES:(g + 1) * TILES, :]).then_inc(s_out, 16)
            sp.wait_ge(s_out, 16 * GROUPS)

        @block.gpsimd
        def _(pool):
            pool.memset(VB[:, :, :], 0.0).then_inc(s_init, 1)
            pool.memset(masked, MASKED).then_inc(s_init, 1)
            pool.memset(minus_half, -0.5).then_inc(s_init, 1)
            pool.wait_ge(s_init, 3)
            pool.wait_ge(s_const, 5 * 16)

            def make_kbd(unit):
                task, r = unit.task, unit.kbd
                pool.wait_ge(s_rope, task.rope_done)
                if r >= 2:
                    pool.wait_ge(full["sc"], hd_units[r - 2].b.sc[1].n + 1)
                if st.kind == "A" and st.task.stage == 3:
                    pool.wait_ge(full["sc"], st.sc_before)
                    pool.wait_ge(by_dve["sc"], plan.rings["sc"][st.sc_before - 1].dve)
                b = unit.i
                pool.tensor_tensor(Kbd[:, r % 2, :].rearrange("p (g k) -> p g k", g=8),
                                   KT[:, b * SEQ:(b + 1) * SEQ].unsqueeze(1).to_broadcast([P, 8, SEQ]),
                                   own_head.unsqueeze(2).to_broadcast([P, 8, SEQ]),
                                   ALU.mult).then_inc(s_kbd, 1)

            for st in steps:
                if st.kind == "A" and st.task.kind != CROSS1:
                    for i, u in enumerate(st.q + st.k):
                        r = st.rope + i
                        pool.wait_ge(by_act["pp"], u.act)
                        sinv = (blocked(sinT[:, st.task.group * GT:(st.task.group + 1) * GT], GB)
                                if st.task.kind == CROSS0
                                else rope16[:, 1, :].unsqueeze(1).to_broadcast([P, GB, SEQ]))
                        sw3 = blocked(SW[:, r % 2, :], GB)
                        pool.tensor_tensor(sw3, sw3, sinv, ALU.mult).then_inc(s_swsin, 1)
                        dst = QT[:, :, i, :] if i < 4 else blocked(KT, GB)
                        pool.wait_ge(s_swsin, r + 1)
                        pool.wait_ge(by_dve["pp"], u.dve)
                        pool.tensor_tensor(dst, dst, sw3, ALU.add).then_inc(s_rope, 1)
                    if st.task.kind == HD16:
                        make_kbd(next(u for u in units if u.task is st.task))
                if st.kind == "B":
                    unit = st.unit
                    if unit.task.kind == HD16:
                        if not unit.last:
                            make_kbd(units[unit.n + 1])
                        for i in range(2):
                            n = 2 * unit.n + i
                            e3 = E[:, n % 4, :].rearrange("p (g k) -> p g k", g=8)
                            pool.wait_ge(s_max, n + 1)
                            pool.tensor_tensor(e3, e3, mx[:, n % 4, :].unsqueeze(2).to_broadcast([P, 8, SEQ]),
                                               ALU.subtract).then_inc(s_sub, 1)
                    blocks = 4 if unit.task.kind == CROSS1 else 8
                    for i in range(2):
                        n = 2 * unit.n + i
                        e3 = E[:, n % 4, :].rearrange("p (g k) -> p g k", g=blocks)
                        pool.wait_ge(s_rinv, n + 1)
                        pool.tensor_tensor(e3, e3, rinv[:, n % 4, 0:blocks].unsqueeze(2).to_broadcast([P, blocks, 512 // blocks]),
                                           ALU.mult).then_inc(s_prob, 1)
                if st.kind == "LN":
                    pool.wait_ge(s_mv, st.n + 1)
                    pool.tensor_scalar(vareps, meanvar[:, :, 1], EPS, None, ALU.add).then_inc(s_ve, 1)
                    pool.wait_ge(s_ve, st.n + 1)
                    pool.tensor_tensor(rstd, vareps, minus_half, ALU.pow).then_inc(s_rstd, 1)

        @block.scalar
        def _(act):
            def make_vbd(unit):
                r = unit.kbd
                read(act, "pp", unit.task.a.v[0])
                if r >= 2:
                    act.wait_ge(full["ou"], hd_units[r - 2].c.ou[0].n + 1)
                src = v_buf(unit.task).rearrange("p (b g e d) -> p b g e d", b=GB, g=4, e=2)
                for half in range(2):
                    rows = slice(64 * half, 64 * half + 64)
                    row = VB[rows, r % 2, :]
                    dst = bass.AP(row.tensor, row.offset + 16 * half, [list(row.ap[0]), [2 * 16 + P, 4], [1, 16]])
                    ins = act.activation(dst, src[rows, unit.i, :, half, :], ACT.Copy)
                ins.then_inc(s_vbd, 1)

            act.wait_ge(s_init, 3)
            for st in steps:
                if st.kind in ("POS", "Z"):
                    u = st.pp[0]
                    act.wait_ge(full["pp"], u.n + 1)
                    rows = slice(0, RANK if st.kind == "Z" else P)
                    at = st.group * GT
                    act.activation(AUX[rows, at:at + GT], bank("pp", u)[rows, :], ACT.Copy).then_inc(by_act["pp"], 1)
                if st.kind == "A":
                    task = st.task
                    if task.kind != CROSS1:
                        for i, u in enumerate(st.q + st.k):
                            r = st.rope + i
                            act.wait_ge(full["pp"], u.n + 1)
                            if r >= 2:
                                act.wait_ge(s_rope, r - 1)
                            act.activation(SW[0:64, r % 2, :], bank("pp", u)[64:P, :], ACT.Copy)
                            act.activation(SW[64:P, r % 2, :], bank("pp", u)[0:64, :], ACT.Copy).then_inc(by_act["pp"], 1)
                    else:
                        act.wait_ge(full["sc"], st.sc_before)
                        act.wait_ge(s_kbd, st.kbd_before)
                        for i, u in list(enumerate(st.q + st.k))[0::2]:
                            act.wait_ge(full["pp"], u.n + 1)
                            dst = QT[0:96, :, i, :] if i < 4 else blocked(KT1[0:96, (i - 4) * 512:(i - 3) * 512], GB)
                            act.activation(dst, blocked(bank("pp", u)[0:96, :], GB),
                                           ACT.Copy).then_inc(by_act["pp"], 1)
                    values_free(act, task)
                    v = v_buf(task)
                    for i, u in enumerate(st.v):
                        act.wait_ge(full["pp"], u.n + 1)
                        ps = bank("pp", u)
                        if task.kind == HD16:
                            v4 = v.rearrange("p (b e f) -> p b e f", e=2, f=P)
                            p3 = ps[:, :].rearrange("p (b f) -> p b f", f=P)
                            act.activation(v4[0:64, :, 0, :], p3[0:64], ACT.Copy)
                            act.activation(v4[64:P, :, 1, :], p3[64:P], ACT.Copy).then_inc(by_act["pp"], 1)
                        elif task.kind == CROSS0:
                            act.activation(v[:, 0:512], ps[:, :], ACT.Copy).then_inc(by_act["pp"], 1)
                        elif u.act is not None:
                            act.activation(v[:, i * 384:(i + 1) * 384], ps[:, 0:384], ACT.Copy).then_inc(by_act["pp"], 1)
                if st.kind == "B":
                    unit = st.unit
                    if unit.task.kind == HD16:
                        make_vbd(unit)
                    for i, u in enumerate(st.sc):
                        n = 2 * unit.n + i
                        if unit.task.kind == HD16:
                            act.wait_ge(s_sub, 2 * unit.kbd + i + 1)
                        else:
                            act.wait_ge(by_dve["sc"], u.dve)
                        act.activation(E[:, n % 4, :], E[:, n % 4, :], ACT.Exp,
                                       scale=SCALE[unit.task.kind]).then_inc(s_exp, 1)
                if st.kind == "T":
                    unit = st.unit
                    if unit.n >= 2:
                        act.wait_ge(full["ou"], units[unit.n - 2].c.ou[-1].n + 1)
                    if unit.task.kind == CROSS0:
                        act.wait_ge(s_amask, 1)
                    for i, u in enumerate(st.tr):
                        act.wait_ge(full["tr"], u.n + 1)
                        if unit.task.kind == CROSS1:
                            dst = PT[:, unit.n % 2, i * 512:(i + 1) * 512]
                            src = bank("tr", u)[:, :]
                        else:
                            dst = PT[:, unit.n % 2, :].rearrange("p (b h q) -> p b h q", b=4, h=2)[:, :, i, :]
                            src = bank("tr", u)[:, :].rearrange("p (b q) -> p b q", b=4)
                        act.activation(dst, src, ACT.Copy).then_inc(by_act["tr"], 1)
                if st.kind == "C":
                    unit = st.unit
                    task = unit.task
                    if unit.first and task.n:
                        act.wait_ge(full["ou"], before(task).d.ou[-1].n + 1)
                    for i, u in enumerate(st.ou):
                        act.wait_ge(full["ou"], u.n + 1)
                        ps = bank("ou", u)
                        if task.kind == HD16:
                            dst = OT[:, :, unit.i * SEQ:(unit.i + 1) * SEQ]
                            src = ps[:, 0:256].rearrange("p (h q) -> p h q", h=4)
                        elif task.kind == CROSS0:
                            m = i // 2
                            dst = OT[:, :, 256 * m:256 * m + 256].rearrange(
                                "p h (x e q) -> p e x h q", x=2, e=2)[:, i % 2]
                            src = ps[:, :].rearrange("p (x h q) -> p x h q", x=2, h=4)
                        else:
                            b = 4 * unit.i + 2 * i
                            dst = OT[0:96, :, b * SEQ:(b + 2) * SEQ].rearrange("p h (b q) -> p b h q", b=2)
                            src = ps[0:96, :].rearrange("p (b h q) -> p b h q", b=2, h=4)
                        act.activation(dst, src, ACT.Copy).then_inc(by_act["ou"], 1)
                if st.kind == "LNT":
                    for i, u in enumerate(st.tr):
                        act.wait_ge(full["tr"], u.n + 1)
                        b = st.group * GB + 2 * i
                        if st.stage < 3:
                            dst = HT[:, :, TOK + b * SEQ:TOK + (b + 2) * SEQ]
                            src = bank("tr", u)[:, :].rearrange("p (c n) -> p c n", c=KC)
                        else:
                            dst = paired[:, :, b:b + 2, 1, :]
                            src = bank("tr", u)[:, :].rearrange("p (c b s) -> p c b s", c=KC, b=2)
                        act.activation(dst, src, ACT.Copy).then_inc(by_act["tr"], 1)
                if st.kind == "F1":
                    task = st.task
                    if task.n >= 2:
                        act.wait_ge(by_dve["sc"], ffn_tasks[task.n - 2].f3.sc[1].dve)
                    act.wait_ge(full["pp"], st.pp[0].n + 1)
                    act.activation(relu[:, task.n % 2, 0, :], bank("pp", st.pp[0])[:, :],
                                   ACT.Relu).then_inc(by_act["pp"], 1)
                if st.kind == "F2":
                    task = st.task
                    if task.n:
                        act.wait_ge(full["sc"], ffn_tasks[task.n - 1].f3.sc[1].n + 1)
                    for c, u in enumerate(st.tr):
                        act.wait_ge(full["tr"], u.n + 1)
                        act.activation(chosenT[:, c, :], bank("tr", u)[:, 0:256].bitcast(BF16),
                                       ACT.Copy).then_inc(by_act["tr"], 1)
                if st.kind == "G1":
                    task = st.task
                    if task.n >= 2:
                        act.wait_ge(by_dve["sc"], gate_tasks[task.n - 2].g1.up[1].dve)
                    for c, u in enumerate(st.gate):
                        act.wait_ge(full["pp"], u.n + 1)
                        act.activation(silu[:, task.n % 2, c, :], bank("pp", u)[:, :],
                                       ACT.Silu).then_inc(by_act["pp"], 1)

        @block.vector
        def _(dve):
            ops = [0]

            def then_wait(ins, s, n):
                ins.then_inc(s, 1)
                dve.wait_ge(s, n)

            dve.wait_ge(s_pos, 32)
            wrap = onehot.rearrange("p r n -> p (r n)")
            for i in range(2):
                part = slice(i * 1024, (i + 1) * 1024)
                then_wait(dve.tensor_scalar(wrap, posi[:, part], 0.0, float(POSITIONS), ALU.is_lt, ALU.mult), s_posf, 3 * i + 1)
                then_wait(dve.tensor_tensor(posf[:, part], posi[:, part], wrap, ALU.add), s_posf, 3 * i + 2)
                then_wait(dve.tensor_scalar(posf[:, part], posf[:, part], 0.0, POSITIONS - 1.0, ALU.max, ALU.min), s_posf, 3 * i + 3)
            dve.wait_ge(s_const, 5 * 16)
            dve.wait_ge(s_init, 3)
            chain = [0]

            def dequantise(p):
                m, k = divmod(p, per_matrix)
                s, which = divmod(m, 3)
                acc = dq[s % 2][:, 1024 * which:1024 * which + 1024]

                def link(ins):
                    chain[0] += 1
                    ins.then_inc(s_dqe, 1)

                if chain[0]:
                    dve.wait_ge(s_dqe, chain[0])
                if k == 0:
                    if m:
                        dve.wait_ge(s_dqd, m)
                    dve.wait_ge(s_dqq, 16 * (m + 1))
                    dve.tensor_copy(dq_b, dq_q).then_inc(s_dqb, 1)
                    return
                code = CODES_USED[k - 1]
                if k == 1:
                    dve.wait_ge(s_dqb, m + 1)
                    if s >= 2:
                        if which < 2:
                            g1 = gate_tasks[GROUPS * (s - 1) - 1].g1
                            dve.wait_ge(full["pp"], g1.gate[1].n + 1)
                            dve.wait_ge(full["sc"], g1.up[1].n + 1)
                        else:
                            dve.wait_ge(full["ou"], gate_tasks[GROUPS * (s - 1) - 1].g2.ou[-1].n + 1)
                    elif s == 1:
                        dve.wait_ge(full["ou"], plan.set_done[n_sets - 2])
                    link(dve.tensor_scalar(acc, dq_b, float(code), float(CODE[code]), ALU.is_equal, ALU.mult))
                    return
                link(dve.tensor_scalar(dq_e, dq_b, float(code), None, ALU.is_equal))
                dve.wait_ge(s_dqe, chain[0])
                link(dve.scalar_tensor_tensor(out=acc, in0=dq_e, scalar=float(CODE[code]), in1=acc,
                                              op0=ALU.mult, op1=ALU.add))
                if k == per_matrix - 1:
                    dve.wait_ge(s_dqe, chain[0])
                    dve.wait_ge(s_dqs, 32 * (m + 1))
                    dve.tensor_tensor(acc, acc, dq_s, ALU.mult).then_inc(s_dqd, 1)

            def pieces(st, a, b):
                for p in range(st.pieces[0] + a, min(st.pieces[0] + b, st.pieces[1])):
                    dequantise(p)

            for st in steps:
                if st.kind == "POS":
                    for k in range(4):
                        n = 4 * st.group + k
                        if n >= 2:
                            g, j = divmod(n - 2, 4)
                            if j < 3:
                                dve.wait_ge(s_ohused, 3 * g + j + 1)
                            else:
                                dve.wait_ge(full["pp"], 2 * g + 2)
                        dve.tensor_scalar(onehot[:, n % 2, :], posf[:, st.group * GT:(st.group + 1) * GT],
                                          iota[:, k:k + 1], None, ALU.is_equal).then_inc(s_oh, 1)
                    u = st.pp[1]
                    dve.wait_ge(full["pp"], u.n + 1)
                    dve.tensor_copy(sinT[:, st.group * GT:(st.group + 1) * GT], bank("pp", u)[:, :]).then_inc(by_dve["pp"], 1)
                if st.kind == "FC":
                    dve.wait_ge(full["tr"], st.tr_before)
                    dve.tensor_copy(ident_b, ident[:, :]).then_inc(s_fcb, 1)
                    dve.wait_ge(s_fc, 48)
                    dve.tensor_copy(ties, ties_f).then_inc(s_fcb, 1)
                if st.kind == "MASK":
                    dve.wait_ge(s_mraw, 32)
                    dve.wait_ge(full["sc"], st.sc_before)
                    dve.tensor_scalar(amask, mask_raw, 0.0, None, ALU.is_equal).then_inc(s_amask, 1)
                if st.kind == "A":
                    task = st.task
                    if st.sc_before:
                        dve.wait_ge(full["sc"], st.sc_before)
                    if st.tr_before:
                        dve.wait_ge(full["tr"], st.tr_before)
                    if st.kbd_before:
                        dve.wait_ge(s_kbd, st.kbd_before)
                    cosv = (blocked(cosT[:, task.group * GT:(task.group + 1) * GT], GB) if task.kind == CROSS0
                            else rope16[:, 0, :].unsqueeze(1).to_broadcast([P, GB, SEQ]))
                    if task.kind == CROSS0 and task.first:
                        dve.wait_ge(by_act["pp"], GROUPS)
                    for i, u in enumerate(st.q + st.k):
                        ps = bank("pp", u)
                        if task.kind == CROSS1:
                            if u.dve is not None:
                                dve.wait_ge(full["pp"], u.n + 1)
                                dst = QT[0:96, :, i, :] if i < 4 else blocked(KT1[0:96, (i - 4) * 512:(i - 3) * 512], GB)
                                dve.tensor_copy(dst, blocked(ps[0:96, :], GB)).then_inc(by_dve["pp"], 1)
                            continue
                        dve.wait_ge(by_act["pp"], u.act)
                        dst = QT[:, :, i, :] if i < 4 else blocked(KT, GB)
                        dve.tensor_tensor(dst, blocked(ps[:, :], GB), cosv, ALU.mult).then_inc(by_dve["pp"], 1)
                    values_free(dve, task)
                    v = v_buf(task)
                    for i, u in enumerate(st.v):
                        ps = bank("pp", u)
                        if u.dve is None:
                            continue
                        dve.wait_ge(full["pp"], u.n + 1)
                        if task.kind == HD16:
                            dve.wait_ge(by_act["pp"], u.act)
                            v4 = v.rearrange("p (b e f) -> p b e f", e=2, f=P)
                            p3 = ps[:, :].rearrange("p (b f) -> p b f", f=P)
                            dve.tensor_copy(v4[0:64, :, 1, :], p3[64:P])
                            dve.tensor_copy(v4[64:P, :, 0, :], p3[0:64]).then_inc(by_dve["pp"], 1)
                        else:
                            dve.tensor_copy(v[:, i * 384:(i + 1) * 384], ps[:, 0:384]).then_inc(by_dve["pp"], 1)
                if st.kind == "B":
                    unit = st.unit
                    kind = unit.task.kind
                    blocks = 4 if kind == CROSS1 else 8

                    def head(i):
                        n = 2 * unit.n + i
                        u = st.sc[i]
                        ps = bank("sc", u)
                        e = E[:, n % 4, :]
                        dve.wait_ge(full["sc"], u.n + 1)
                        if unit.n >= 2:
                            dve.wait_ge(full["tr"], units[unit.n - 2].t.tr[i].n + 1)
                        if kind == HD16:
                            dve.tensor_tensor(blocked(e, 8), blocked(ps[:, :], 8),
                                              causal[:, :].unsqueeze(1).to_broadcast([P, 8, SEQ]),
                                              ALU.add).then_inc(by_dve["sc"], 1)
                            dve.wait_ge(by_dve["sc"], u.dve)
                            dve.tensor_reduce(mx[:, n % 4, :], blocked(e, 8), AX.X, ALU.max).then_inc(s_max, 1)
                            return
                        if kind == CROSS0:
                            if unit.task.first and i == 0:
                                dve.wait_ge(s_amask, 1)
                            g = unit.task.group
                            dve.copy_predicated(ps[:, :], amask[:, g * GT:(g + 1) * GT],
                                                masked[:, 0:1].to_broadcast([P, 512])).then_inc(s_pred, 1)
                            dve.wait_ge(s_pred, 2 * (unit.task.n - cross0_first) + i + 1)
                        dve.tensor_reduce(mx[:, n % 4, 0:blocks], blocked(ps[:, :], blocks), AX.X, ALU.max).then_inc(s_max, 1)
                        dve.wait_ge(s_max, n + 1)
                        dve.tensor_tensor(blocked(e, blocks), blocked(ps[:, :], blocks),
                                          mx[:, n % 4, 0:blocks].unsqueeze(2).to_broadcast([P, blocks, 512 // blocks]),
                                          ALU.subtract).then_inc(by_dve["sc"], 1)

                    def tail(i):
                        n = 2 * unit.n + i
                        dve.wait_ge(s_exp, n + 1)
                        dve.tensor_reduce(sums[:, n % 4, 0:blocks], blocked(E[:, n % 4, :], blocks), AX.X,
                                          ALU.add).then_inc(s_sum, 1)
                        dve.wait_ge(s_sum, n + 1)
                        dve.reciprocal(rinv[:, n % 4, 0:blocks], sums[:, n % 4, 0:blocks]).then_inc(s_rinv, 1)

                    head(0)
                    head(1)
                    pieces(st, 0, 2)
                    tail(0)
                    tail(1)
                if st.kind in ("D", "F4", "G2"):
                    task = st.task
                    if task.stage == 0 and task.group == 0:
                        dve.wait_ge(s_x, 16 * GROUPS)
                    if st.ou[0].dve > 1:
                        dve.wait_ge(by_dve["ou"], st.ou[0].dve - 1)
                    if task.first and task.stage:
                        dve.wait_ge(s_xn, TILES * GROUPS * task.stage - TILES * (GROUPS - 1))
                    for i, u in enumerate(st.ou):
                        tile = task.group * TILES + i
                        dve.wait_ge(full["ou"], u.n + 1)
                        dve.tensor_tensor(X[:, tile, :], X[:, tile, :], bank("ou", u)[:, :],
                                          ALU.add).then_inc(by_dve["ou"], 1)
                        if st.kind == "G2":
                            pieces(st, 3 * i, 3 * i + 3)
                if st.kind == "LN":
                    dve.wait_ge(by_dve["ou"], st.added)
                    if st.n:
                        dve.wait_ge(s_xn, TILES * st.n)
                    for i in range(TILES):
                        dve.bn_stats(stats[:, i, :], X[:, st.group * TILES + i, :]).then_inc(s_stat, 1)
                    for i in range(TILES):
                        dve.wait_ge(s_stat, TILES * st.n + i + 1)
                        ins = dve.bn_aggr(meanvar[:, i, :], stats[:, i, :])
                    ins.then_inc(s_mv, 1)
                    dve.wait_ge(s_mv, st.n + 1)
                    dve.wait_ge(s_rstd, st.n + 1)
                    for i in range(TILES):
                        tile = st.group * TILES + i
                        dve.tensor_scalar(X[:, tile, :], X[:, tile, :], meanvar[:, i, 0:1], rstd[:, i:i + 1],
                                          ALU.subtract, ALU.mult).then_inc(s_xn, 1)
                if st.kind == "F1":
                    task = st.task
                    for i2, u in enumerate(st.sc):
                        n = 2 * task.n + i2
                        dve.wait_ge(full["sc"], u.n + 1)
                        ps = blocked(bank("sc", u)[:, :], 16)
                        mxb = blkmax[:, 2 * (n % 2):2 * (n % 2) + 2, :].rearrange("p a b -> p (a b)")
                        dve.tensor_reduce(mxb, ps, AX.X, ALU.max).then_inc(s_bmax, 1)
                        dve.wait_ge(s_bmax, n + 1)
                        if task.n >= 2:
                            dve.wait_ge(full["tr"], ffn_tasks[task.n - 2].f2.tr[1].n + 1)
                        dst = chosen[:, task.n % 2, 2 * i2:2 * i2 + 2, :].rearrange("p i (g k) -> p (i g) k", k=BLK)
                        dve.tensor_tensor(dst, ps, mxb.unsqueeze(2).to_broadcast([P, 16, BLK]),
                                          ALU.is_ge).then_inc(by_dve["sc"], 1)
                    if task.n >= 2:
                        dve.wait_ge(by_dve["sc"], ffn_tasks[task.n - 2].f3.sc[1].dve)
                    dve.wait_ge(full["pp"], st.pp[1].n + 1)
                    dve.tensor_scalar(relu[:, task.n % 2, 1, :], bank("pp", st.pp[1])[:, :], 0.0, None,
                                      ALU.max).then_inc(by_dve["pp"], 1)
                if st.kind == "F3":
                    task = st.task
                    read(dve, "pp", *task.f1.pp)
                    if task.n:
                        dve.wait_ge(full["ou"], ffn_tasks[task.n - 1].f4.ou[-1].n + 1)
                    for c, u in enumerate(st.sc):
                        dve.wait_ge(full["sc"], u.n + 1)
                        dve.scalar_tensor_tensor(out=hsel[:, c, :], in0=bank("sc", u)[:, :], scalar=-TIE,
                                                 in1=relu[:, task.n % 2, c, :], op0=ALU.is_equal,
                                                 op1=ALU.mult).then_inc(by_dve["sc"], 1)
                if st.kind == "G1":
                    task = st.task
                    if task.n >= 2:
                        dve.wait_ge(full["ou"], gate_tasks[task.n - 2].g2.ou[-1].n + 1)
                    for c, u in enumerate(st.up):
                        dve.wait_ge(full["sc"], u.n + 1)
                        dve.wait_ge(by_act["pp"], st.gate[c].act)
                        dve.tensor_tensor(hgate[:, task.n % 2, c, :], bank("sc", u)[:, :],
                                          silu[:, task.n % 2, c, :], ALU.mult).then_inc(by_dve["sc"], 1)

        @block.tensor
        def _(pe):
            def take(ring, u):
                if u.n >= 2:
                    old = plan.rings[ring][u.n - 2]
                    if old.act is not None:
                        pe.wait_ge(by_act[ring], old.act)
                    if old.dve is not None:
                        pe.wait_ge(by_dve[ring], old.dve)
                return bank(ring, u)

            def turned(stage, group):
                if stage == 0:
                    pe.wait_ge(s_ht, 16 * KC)
                else:
                    pe.wait_ge(by_act["tr"], plan.turned[GROUPS * (stage - 1) + group].tr[-1].act)

            def product(ps, pairs):
                for i, (lhsT, rhs) in enumerate(pairs):
                    ins = pe.matmul(ps, lhsT, rhs, start=i == 0, stop=i == len(pairs) - 1)
                return ins

            pe.wait_ge(s_const, 5 * 16)
            for st in steps:
                if st.kind == "POS":
                    pe.wait_ge(s_pos, 32)
                    ps = [take("pp", u) for u in st.pp]
                    for k in range(4):
                        pe.wait_ge(s_oh, 4 * st.group + k + 1)
                        for i in range(2):
                            ins = pe.matmul(ps[i][:, :], ptab[:, k, i * P:(i + 1) * P],
                                            onehot[:, (4 * st.group + k) % 2, :], start=k == 0, stop=k == 3)
                            if k == 3:
                                ins.then_inc(full["pp"], 1)
                        if k < 3:
                            ins.then_inc(s_ohused, 1)
                if st.kind == "A":
                    task = st.task
                    pe.wait_ge(s_w[task.wset % 2], loaded[task.wset])
                    turned(task.stage, task.group)
                    if task.kind == CROSS0:
                        pe.wait_ge(s_ctx, 16 * KC)
                    if task.kind == CROSS1:
                        pe.wait_ge(s_paired[task.group], 16 * KC)
                    wq, wk, wv, _ = weights(task.kind, task.wset)
                    head = 96 if task.kind == CROSS1 else P
                    for j, u in enumerate(st.q):
                        ps = take("pp", u)
                        product(ps[0:head, :], [(wq[:, c, j * head:(j + 1) * head], x_cols(task.stage, c, task.group))
                                                for c in range(KC)]).then_inc(full["pp"], 1)
                    first = task.group * GT + (TOK if task.kind == HD16 else 0)
                    for i, u in enumerate(st.k):
                        ps = take("pp", u)
                        if task.kind == CROSS1:
                            b = task.group * GB + 4 * i
                            rhs = [HT[:, c, b * P:(b + 4) * P] for c in range(KC)]
                        else:
                            rhs = [HT[:, c, first:first + GT] for c in range(KC)]
                        product(ps[0:head, :], [(wk[:, c, :], rhs[c]) for c in range(KC)]).then_inc(full["pp"], 1)
                    for i, u in enumerate(st.v):
                        ps = take("pp", u)
                        for n in range(4):
                            if task.kind == CROSS1:
                                b = task.group * GB + 4 * i + n
                                ins = product(ps[:, n * 96:(n + 1) * 96],
                                              [(HT[:, c, b * P:(b + 1) * P], wv[:, c, :]) for c in range(KC)])
                            else:
                                at = first + n * P
                                ins = product(ps[:, n * P:(n + 1) * P],
                                              [(HT[:, c, at:at + P], wv[:, c, :]) for c in range(KC)])
                        ins.then_inc(full["pp"], 1)
                if st.kind == "B":
                    unit = st.unit
                    task = unit.task
                    if task.kind == CROSS1:
                        read(pe, "pp", *task.a.k)
                    else:
                        pe.wait_ge(s_rope, task.rope_done)
                    for i, u in enumerate(st.sc):
                        ps = take("sc", u)
                        if task.kind == HD16:
                            pe.wait_ge(s_kbd, unit.kbd + 1)
                            b = unit.i
                            ins = pe.matmul(ps[:, :], QT[:, b, 2 * i:2 * i + 2, :],
                                            Kbd[:, unit.kbd % 2, :], start=True, stop=True)
                        elif task.kind == CROSS0:
                            for b in range(GB):
                                cols = slice(b * SEQ, (b + 1) * SEQ)
                                ins = pe.matmul(ps[:, cols], QT[:, b, 2 * i:2 * i + 2, :], KT[:, cols],
                                                start=True, stop=True)
                        else:
                            for e in range(2):
                                for h in range(2):
                                    b = 4 * unit.i + 2 * i + e
                                    at = (2 * e + h) * P
                                    ins = pe.matmul(ps[:, at:at + P],
                                                    QT[0:96, b, 2 * h:2 * h + 2, :],
                                                    KT1[0:96, b * P:(b + 1) * P], start=True, stop=True)
                        ins.then_inc(full["sc"], 1)
                if st.kind == "T":
                    unit = st.unit
                    for i, u in enumerate(st.tr):
                        n = 2 * unit.n + i
                        ps = take("tr", u)
                        pe.wait_ge(s_prob, n + 1)
                        for b in range(4):
                            ins = pe.transpose(ps[:, b * P:(b + 1) * P], E[:, n % 4, b * P:(b + 1) * P], ident[:, :])
                        ins.then_inc(full["tr"], 1)
                if st.kind == "C":
                    unit = st.unit
                    task = unit.task
                    pe.wait_ge(by_act["tr"], unit.t.tr[1].act)
                    read(pe, "pp", *task.a.v)
                    v = v_buf(task)
                    pt = PT[:, unit.n % 2, :]
                    if task.kind == CROSS0:
                        for m in range(2):
                            ps = [take("ou", u) for u in st.ou[2 * m:2 * m + 2]]
                            for x in range(2):
                                for e in range(2):
                                    i = 2 * m + x
                                    rows = slice(64 * e, 64 * e + 64)
                                    ins = pe.matmul(ps[e][:, x * 256:(x + 1) * 256], v[rows, i * P:(i + 1) * P],
                                                    pt[rows, i * 256:(i + 1) * 256], start=True, stop=True)
                                    if x:
                                        ins.then_inc(full["ou"], 1)
                        continue
                    for i, u in enumerate(st.ou):
                        ps = take("ou", u)
                        if task.kind == HD16:
                            pe.wait_ge(s_vbd, unit.kbd + 1)
                            ins = product(ps[:, 0:256], [(VB[:, unit.kbd % 2, g * P:(g + 1) * P],
                                                          pt[:, g * 256:(g + 1) * 256]) for g in range(4)])
                        else:
                            for e in range(2):
                                b = 4 * unit.i + 2 * i + e
                                at = (2 * i + e) * 256
                                ins = pe.matmul(ps[0:96, e * 256:(e + 1) * 256], v[:, b * 96:(b + 1) * 96],
                                                pt[:, at:at + 256], start=True, stop=True)
                        ins.then_inc(full["ou"], 1)
                if st.kind == "D":
                    task = st.task
                    rows = 96 if task.kind == CROSS1 else P
                    wo = weights(task.kind, task.wset)[3]
                    pe.wait_ge(by_act["ou"], plan.rings["ou"][task.c_done - 1].act)
                    for i, u in enumerate(st.ou):
                        ps = take("ou", u)
                        product(ps[:, :], [(OT[0:rows, j, i * P:(i + 1) * P], wo[:, j, :])
                                           for j in range(4)]).then_inc(full["ou"], 1)
                if st.kind == "LNT":
                    for i, u in enumerate(st.tr):
                        ps = take("tr", u)
                        pe.wait_ge(s_xn, TILES * st.n + i + 1)
                        for c in range(KC):
                            ins = pe.transpose(ps[:, c * P:(c + 1) * P],
                                               X[:, st.group * TILES + i, c * P:(c + 1) * P], ident[:, :])
                        ins.then_inc(full["tr"], 1)
                if st.kind == "Z":
                    pe.wait_ge(s_fc, 48)
                    pe.wait_ge(s_fcb, 2)
                    turned(2, st.group)
                    ps = take("pp", st.pp[0])
                    product(ps[0:RANK, :], [(c1_sb[:, c, :], x_cols(2, c, st.group))
                                            for c in range(KC)]).then_inc(full["pp"], 1)
                if st.kind == "F1":
                    task = st.task
                    sub = task.sub
                    w1, _ = ffn_weights(wslot(task.wset))
                    if sub == 0:
                        z = next(s for s in steps if s.kind == "Z" and s.group == task.group)
                        read(pe, "pp", z.pp[0])
                    for i2, u in enumerate(st.sc):
                        ps = take("sc", u)
                        for e in range(2):
                            at = task.group * GT + (2 * i2 + e) * P
                            ins = pe.matmul(ps[:, e * ROW:(e + 1) * ROW], zT[:, at:at + P],
                                            c2_sb[:, sub * ROW:(sub + 1) * ROW], start=True, stop=True)
                        ins.then_inc(full["sc"], 1)
                    pe.wait_ge(s_w[task.wset % 2], loaded[task.wset])
                    for c, u in enumerate(st.pp):
                        ps = take("pp", u)
                        product(ps[:, :], [(w1[:, k, c * P:(c + 1) * P], x_cols(2, k, task.group))
                                           for k in range(KC)]).then_inc(full["pp"], 1)
                if st.kind == "F2":
                    task = st.task
                    pe.wait_ge(by_dve["sc"], task.f1.sc[1].dve)
                    for c, u in enumerate(st.tr):
                        ps = take("tr", u)[:, 0:256].bitcast(BF16)
                        for i in range(TILES):
                            ins = pe.transpose(ps[:, i * P:(i + 1) * P], chosen[:, task.n % 2, i, c * P:(c + 1) * P],
                                               ident_b)
                        ins.then_inc(full["tr"], 1)
                if st.kind == "F3":
                    task = st.task
                    for c, u in enumerate(st.sc):
                        ps = take("sc", u)
                        pe.wait_ge(by_act["tr"], task.f2.tr[c].act)
                        pe.matmul(ps[:, :], ties, chosenT[:, c, :], start=True, stop=True).then_inc(full["sc"], 1)
                if st.kind == "F4":
                    task = st.task
                    _, w2 = ffn_weights(wslot(task.wset))
                    pe.wait_ge(by_dve["sc"], task.f3.sc[1].dve)
                    for i, u in enumerate(st.ou):
                        ps = take("ou", u)
                        product(ps[:, :], [(hsel[:, c, i * P:(i + 1) * P], w2[:, c, :])
                                           for c in range(2)]).then_inc(full["ou"], 1)
                if st.kind == "G1":
                    task = st.task
                    if task.sub == 0:
                        turned(5, task.group)
                    pe.wait_ge(s_dqd, 3 * task.sub + 2)
                    mats = [dq[task.sub % 2][:, 1024 * m:1024 * m + 1024].rearrange("p (c n) -> p c n", c=KC)
                            for m in range(2)]
                    for c in range(2):
                        for ring, u, w in (("pp", st.gate[c], mats[0]), ("sc", st.up[c], mats[1])):
                            ps = take(ring, u)
                            product(ps[:, :], [(w[:, k, c * P:(c + 1) * P], x_cols(5, k, task.group))
                                               for k in range(KC)]).then_inc(full[ring], 1)
                if st.kind == "G2":
                    task = st.task
                    pe.wait_ge(s_dqd, 3 * task.sub + 3)
                    pe.wait_ge(by_dve["sc"], task.g1.up[1].dve)
                    w = dq[task.sub % 2][:, 2048:3072].rearrange("p (c n) -> p c n", c=2)
                    for i, u in enumerate(st.ou):
                        ps = take("ou", u)
                        product(ps[:, :], [(hgate[:, task.n % 2, c, i * P:(i + 1) * P], w[:, c, :])
                                           for c in range(2)]).then_inc(full["ou"], 1)


def constants():
    p = np.arange(P)
    c = {"ident": np.eye(P, dtype=np.float32)}
    c["causal"] = np.where(np.arange(SEQ)[None, :] > (p % SEQ)[:, None], np.float32(FUTURE), np.float32(0))
    c["own_head"] = (((p % 64) // 8)[:, None] == np.arange(8)[None, :]).astype(np.float32)
    c["iota"] = (p[:, None] + P * np.arange(4)[None, :]).astype(np.float32)

    def tables(length, dim):
        inv = (1.0 / np.float32(10000.0) ** (np.arange(0, dim, 2, dtype=np.float32) / np.float32(dim))).astype(np.float32)
        ang = np.outer(np.arange(length, dtype=np.float32), inv).astype(np.float32)
        return np.cos(ang).astype(np.float32), np.sin(ang).astype(np.float32)

    cos, sin = tables(SEQ, 16)
    sign = np.where(p < 64, -1, 1).astype(np.float32)
    c["rope16"] = np.stack([cos.T[p % 8], sin.T[p % 8] * sign[:, None]], 1).astype(np.float32)
    cos, sin = tables(POSITIONS, P)
    c["ptab"] = np.concatenate([cos, cos, -sin, sin], 1).astype(np.float32)
    same = (p[:, None] // BLK) == (p[None, :] // BLK)
    c["ties"] = ((same & (p[:, None] < p[None, :])).astype(np.float32)
                 - np.float32(TIE) * np.eye(P, dtype=np.float32)).astype(np.float32)
    return c


def kernel(**inputs):
    import concourse.bacc as _bacc
    from concourse.bass_utils import run_bass_kernel_spmd as _run

    a = {k: np.asarray(v) for k, v in inputs.items()}
    arrays = {}

    def lay(name, value):
        arrays[name] = np.ascontiguousarray(value)

    lay("x_tok", a["x"].reshape(TOK, DIM))
    lay("x_T", a["x"].reshape(TOK, DIM).T)
    lay("ctx_T", a["ctx_4096"].reshape(TOK, DIM).T)
    lay("pos", a["pos_BxS2"].reshape(1, TOK))
    lay("mask", a["mask_BxSxS2_ik0"])

    def by_half(w, heads):
        w = w.reshape(DIM, 8, heads // 8, 2, 8)
        return w.transpose(0, 2, 3, 1, 4).reshape(DIM, heads * 16)

    def out_rows(w):
        return w.reshape(8, 4, 16, DIM).transpose(1, 0, 2, 3).reshape(DIM, DIM)

    for layer, turn in ((0, True), (1, False)):
        w = {n: a[f"L{layer}_attn_W{n}"] for n in "qkvo"}
        if turn:
            w = {n: v.T for n, v in w.items()}
        lay(f"hd{layer}_q", by_half(w["q"], 32))
        lay(f"hd{layer}_k", by_half(w["k"], 8))
        lay(f"hd{layer}_v", w["v"])
        lay(f"hd{layer}_o", out_rows(w["o"]))
    for n in "qkvo":
        lay(f"cross0_{n}", a[f"L0_xattn_W{n}"])
        lay(f"cross1_{n}", a[f"L1_xattn_W{n}"].T)
    lay("c1T", a["L0_ffn_c1_w"].T)
    lay("c2T", a["L0_ffn_c2_w"].T)
    lay("w1T", a["L0_ffn_w1"].T)
    lay("w2t", a["L0_ffn_w2t"])
    lay("gate_q", a["L1_ffn_gate_q"].T)
    lay("up_q", a["L1_ffn_up_q"].T)
    lay("down_q", a["L1_ffn_down_q"].T)
    lay("gate_s", a["L1_ffn_gate_absmax"].reshape(INTER, DIM // 64).T)
    lay("up_s", a["L1_ffn_up_absmax"].reshape(INTER, DIM // 64).T)
    lay("down_s", a["L1_ffn_down_absmax"].reshape(DIM, INTER // 64).T)
    consts = constants()
    for n, v in consts.items():
        lay(f"const_{n}", v)

    nc = _bacc.Bacc("TRN2", target_bir_lowering=False, num_devices=1)
    d = {n: nc.dram_tensor(n, v.shape, mybir.dt.from_np(v.dtype), kind="ExternalInput").ap() for n, v in arrays.items()}
    out = nc.dram_tensor("out", (TOK, DIM), F32, kind="ExternalOutput").ap()
    decoder_kernel(nc, d["x_tok"], d["x_T"], d["ctx_T"], d["pos"], d["mask"],
                   [[d[f"hd{i}_{n}"] for n in "qkvo"] for i in range(2)],
                   [d[f"cross0_{n}"] for n in "qkvo"],
                   d["c1T"], d["c2T"], d["w1T"], d["w2t"],
                   [d[f"cross1_{n}"] for n in "qkvo"],
                   d["gate_q"], d["gate_s"], d["up_q"], d["up_s"], d["down_q"], d["down_s"],
                   {n: d[f"const_{n}"] for n in consts}, out)
    r = _run(nc, [arrays], core_ids=[0])
    return r.results[0]["out"].reshape(BATCH, SEQ, DIM)
```

```python
from contextlib import ExitStack

import concourse.bass as bass
from concourse import mybir
import numpy as np

ALU = mybir.AluOpType
ACT = mybir.ActivationFunctionType
AX = mybir.AxisListType
F32 = mybir.dt.float32
BF16 = mybir.dt.bfloat16
I32 = mybir.dt.int32
U16 = mybir.dt.uint16

P = 128
BATCH, SEQ, DIM = 32, 64, 512
TOK = BATCH * SEQ
GROUPS = 4
GT = TOK // GROUPS
GB = BATCH // GROUPS
TILES = GT // P
KC = DIM // P
INTER = 1792
ROW = 256
FSETS = INTER // ROW
BLK = 32
RANK = 16
POSITIONS = 512
EPS = 1e-5
CODE = np.array([-1.0, -0.6961928009986877, -0.5250730514526367, -0.39491748809814453,
                 -0.28444138169288635, -0.18477343022823334, -0.09105003625154495, 0.0,
                 0.07958029955625534, 0.16093020141124725, 0.24611230194568634, 0.33791524171829224,
                 0.44070982933044434, 0.5626170039176941, 0.7229568362236023, 1.0], np.float32)
FUTURE = -3.0e38
MASKED = -1.0e9 * float(np.sqrt(128.0))
TIE = 64.0

HD16, CROSS0, CROSS1 = "heads of 16", "cross-attention 0", "cross-attention 1"
SCALE = {HD16: 0.25, CROSS0: 128.0 ** -0.5, CROSS1: 96.0 ** -0.5}
UNITS = {HD16: GB, CROSS0: 1, CROSS1: 2}
PARTS = {CROSS0: [[("q", 0)], [("k", 0)], [("q", 1), ("q", 2), ("q", 3), ("v", 0)]],
         CROSS1: [[("q", 0)], [("q", 1), ("k", 0)], [("k", 1), ("q", 2)], [("v", 0), ("v", 1)]]}
STAGES = [(0, HD16, 1), (1, CROSS0, 8), (2, "ffn0", FSETS), (3, HD16, 1), (4, CROSS1, 4), (5, "ffn1", FSETS)]
CODES_USED = [k for k in range(16) if CODE[k] != 0.0]


class Use:

    def __init__(self, n, act, dve):
        self.n, self.act, self.dve = n, act, dve


class Task:

    def __init__(self, stage, kind, group, sub, wset, last_set, first):
        self.stage, self.kind, self.group, self.sub, self.wset = stage, kind, group, sub, wset
        self.last_set, self.first = last_set, first
        self.last_group = last_set and group == GROUPS - 1
        self.proj = {"q": [], "k": [], "v": []}
        self.quarters = []
        self.d = []


class Unit:

    def __init__(self, task, i, n):
        self.task, self.i, self.n, self.first = task, i, n, i == 0
        self.ou = []
        self.exp_late = False


class Step:

    def __init__(self, kind, plan, task=None, unit=None, group=None, n=None, stage=None, part=None):
        self.kind, self.task, self.unit, self.group, self.n, self.stage = kind, task, unit, group, n, stage
        self.part = part
        self.pp_before, self.sc_before = plan.count("pp"), plan.count("sc")
        self.tr_before, self.ou_before = plan.count("tr"), plan.count("ou")
        self.kbd_before = plan.kbds
        self.ropes_before = plan.ropes
        self.added = plan.read["ou", "dve"]
        self.final = stage == STAGES[-1][0]
        self.pieces = (0, 0)


class Plan:

    def __init__(self):
        self.rings = {r: [] for r in ("pp", "sc", "tr", "ou")}
        self.read = {(r, e): 0 for r in self.rings for e in ("act", "dve")}
        self.steps = []
        self.tasks = self.ropes = self.kbds = self.norms = self.ffns = self.g1s = 0
        self.turns = 0
        self.pos_steps = []
        self.taken = None
        self.set_done = {}
        self.turned = {}
        self.by_unit, self.hd_units = [], []
        self.pending = []
        self.build()
        self.place_dequantising()

    def use(self, ring, readers, count):
        out = []
        for _ in range(count):
            for e in readers:
                self.read[ring, e] += 1
            u = Use(len(self.rings[ring]), self.read[ring, "act"] if "act" in readers else None,
                    self.read[ring, "dve"] if "dve" in readers else None)
            self.rings[ring].append(u)
            out.append(u)
        return out

    def alternate(self, ring, count):
        return [self.use(ring, (("act",), ("dve",))[i % 2], 1)[0] for i in range(count)]

    def count(self, ring):
        return len(self.rings[ring])

    def add(self, kind, **fields):
        s = Step(kind, self, **fields)
        self.steps.append(s)
        return s

    def positions(self, group):
        s = self.add("POS", group=group)
        s.pp = self.use("pp", ("act", "dve"), 1)
        self.pos_steps.append(s)

    def project(self, task, part):
        self.need(task)
        s = self.add("A", task=task, part=part)
        s.items = []
        for what, i in PARTS[task.kind][part]:
            if task.kind == CROSS1:
                readers = (("act",), ("dve",))[self.turns % 2]
                self.turns += 1
            else:
                readers = ("act",) if what == "v" else ("act", "dve")
            u = self.use("pp", readers, 1)[0]
            rope = None
            if task.kind == CROSS0 and what != "v":
                rope = self.ropes
                self.ropes += 1
            s.items.append((what, i, u, rope))
            task.proj[what].append(u)
        task.rope_done = self.ropes

    def quarter(self, task, i):
        self.need(task)
        s = self.add("AQ", task=task, part=i)
        s.q, s.kv = self.use("pp", ("act", "dve"), 2)
        s.rope = self.ropes
        self.ropes += 2
        s.rope_done = self.ropes
        task.quarters.append(s)

    def scores(self, unit):
        s = self.add("B", unit=unit)
        if unit.task.kind == HD16:
            unit.kbd = self.kbds
            self.kbds += 1
            self.hd_units.append(unit)
            unit.task.last_kbd = unit.kbd
            unit.quarter = unit.task.quarters[unit.i // 2]
            unit.rope_done = unit.quarter.rope_done
        else:
            unit.rope_done = unit.task.rope_done
        s.sc = self.use("sc", ("dve",), 2)
        unit.b = s
        self.finish_norm()

    def turn(self, unit):
        s = self.add("T", unit=unit)
        s.tr = self.use("tr", ("act",), 2)
        unit.t = s
        before = self.steps[-2]
        if before.kind == "B" and before.unit.task.kind == HD16:
            before.unit.exp_late = True

    def values(self, unit, part=0):
        s = self.add("C", unit=unit, part=part)
        s.ou = self.use("ou", ("act",), 1 if unit.task.kind == HD16 else 2)
        unit.ou += s.ou

    def output(self, task, tiles):
        s = self.add("D", task=task)
        s.tiles = tiles
        units = [u for u in self.by_unit if u.task is task]
        last = units[2 * tiles[-1] + 1 if task.kind == HD16 else tiles[-1] * len(units) // TILES]
        s.needs = last.ou[-1]
        s.ou = self.use("ou", ("dve",), len(tiles))
        task.d += s.ou
        if tiles[-1] == TILES - 1:
            self.set_done[task.wset] = self.count("ou")
            self.after(task)

    def after(self, task):
        if task.last_set:
            self.finish_norm()
            self.taken = self.add("LS", group=task.group, n=self.norms, stage=task.stage)
            self.norms += 1

    def finish_norm(self):
        if self.taken:
            s = self.taken
            self.pending.append(self.add("LN", group=s.group, n=s.n, stage=s.stage))
            self.taken = None

    def turn_norms(self, keep=0):
        while len(self.pending) > max(keep, 0):
            ln = self.pending.pop(0)
            if not ln.final:
                s = self.add("LNT", group=ln.group, n=ln.n, stage=ln.stage)
                s.tr = self.use("tr", ("act",), TILES)
                self.turned[ln.n] = s

    def need(self, task):
        if self.taken and self.taken.n <= GROUPS * (task.stage - 1) + task.group:
            self.finish_norm()
        while self.pending and self.pending[0].n <= GROUPS * (task.stage - 1) + task.group:
            self.turn_norms(len(self.pending) - 1)

    def heads_of_16(self, units, before_last, normed=None):
        quarters = [(u.task, u.i // 2) for u in units[::2]]
        self.scores(units[0])
        if normed:
            self.after(normed)
        for k, u in enumerate(units):
            if k + 1 < len(units):
                self.scores(units[k + 1])
            else:
                before_last()
            self.turn(u)
            if k % 2 == 0 and k // 2 + 2 < len(quarters):
                self.quarter(*quarters[k // 2 + 2])
            if k % 2 and k >= 3:
                v = units[k - 3]
                self.output(v.task, [v.i // 2])
            elif k % 8 == 6:
                self.turn_norms()
            self.values(u)
            if u.task.stage == 0 and k % 2 and k < 2 * GROUPS:
                self.positions(k // 2)

    def build(self):
        wset = 0
        tasks = {}
        for stage, kind, sets in STAGES:
            tasks[stage] = [Task(stage=stage, kind=kind, group=t, sub=s, wset=wset + s, last_set=s == sets - 1,
                                 first=(s == 0 and t == 0)) for s in range(sets) for t in range(GROUPS)]
            wset += sets
            if kind not in (HD16, CROSS0, CROSS1):
                continue
            for task in tasks[stage]:
                task.n = self.tasks
                self.tasks += 1
                task.units = []
                for i in range(UNITS[kind]):
                    u = Unit(task, i, len(self.by_unit))
                    self.by_unit.append(u)
                    task.units.append(u)

        def units(stage):
            return [u for t in tasks[stage] for u in t.units]

        def project(task, parts):
            for part in parts:
                self.project(task, part)

        c = tasks[1]
        for i in range(2):
            self.quarter(tasks[0][0], i)
        self.heads_of_16(units(0), lambda: project(c[0], range(3)))
        self.add("MASK")
        self.scores(c[0].units[0])
        project(c[1], range(2))
        self.output(tasks[0][-1], [TILES - 1])
        project(c[1], [2])
        for n, task in enumerate(c):
            u = task.units[0]
            self.turn(u)
            if n + 1 < len(c):
                self.scores(c[n + 1].units[0])
            else:
                self.add("FC")
            if n:
                self.output(c[n - 1], list(range(TILES)))
            self.turn_norms(1)
            if n + 2 < len(c):
                self.project(c[n + 2], 0)
            self.values(u, 0)
            if n + 2 < len(c):
                self.project(c[n + 2], 1)
            self.values(u, 1)
            if n + 2 < len(c):
                self.project(c[n + 2], 2)
        self.turn_norms(0)
        self.low_rank(0)
        self.low_rank(1)
        self.output(c[-1], list(range(TILES)))
        self.feed_forward_0(tasks[2], lambda: [self.quarter(tasks[3][0], i) for i in range(2)])
        c = tasks[4]
        self.last_cross = c[-1].wset
        self.heads_of_16(units(3), lambda: [project(c[0], range(4)), self.scores(c[0].units[0])], tasks[2][-1])
        self.scores(c[0].units[1])
        self.output(tasks[3][-1], [TILES - 1])
        for n, task in enumerate(c):
            a, b = task.units
            following = c[n + 1] if n + 1 < len(c) else None

            def ahead(part):
                if following:
                    self.project(following, part)
                else:
                    self.turn_norms(len(self.pending) - 1)

            self.turn(a)
            ahead(0)
            self.values(a)
            ahead(1)
            self.turn(b)
            ahead(2)
            self.values(b)
            if following:
                self.project(following, 3)
                self.scores(following.units[0])
            self.output(task, [0, 1])
            if following:
                self.scores(following.units[1])
            self.output(task, [2, 3])
        self.feed_forward_1(tasks[5])

    def low_rank(self, group):
        s = self.add("Z", group=group)
        s.pp = self.use("pp", ("act",), 1)

    def feed_forward_0(self, tasks, before_last):
        def f1(task):
            if task.sub == 0 and task.group >= 2:
                self.need(task)
                self.low_rank(task.group)
            task.n = self.ffns
            self.ffns += 1
            task.f1 = self.add("F1", task=task)
            task.f1.sc = self.use("sc", ("dve",), 2)
            task.f1.pp = self.alternate("pp", 2)

        def f2(task):
            task.f2 = self.add("F2", task=task)
            task.f2.tr = self.use("tr", ("act",), 2)

        def f3(task):
            task.f3 = self.add("F3", task=task)
            task.f3.sc = self.use("sc", ("dve",), 2)
            self.finish_norm()

        def f4(task):
            task.f4 = self.add("F4", task=task)
            task.f4.ou = self.use("ou", ("dve",), TILES)
            self.set_done[task.wset] = self.count("ou")

        f1(tasks[0])
        for i, task in enumerate(tasks):
            if i + 1 < len(tasks):
                f1(tasks[i + 1])
            f2(task)
            if i:
                f4(tasks[i - 1])
            f3(task)
            if i:
                self.after(tasks[i - 1])
            self.turn_norms(1)
        before_last()
        f4(tasks[-1])

    def feed_forward_1(self, tasks):
        def g1(task):
            self.need(task)
            task.n = self.g1s
            self.g1s += 1
            task.g1 = self.add("G1", task=task)
            task.g1.gate = self.use("pp", ("act",), 2)
            task.g1.up = self.use("sc", ("dve",), 2)
            self.finish_norm()

        def g2(task):
            task.g2 = self.add("G2", task=task)
            task.g2.ou = self.use("ou", ("dve",), TILES)
            self.after(task)
            if task.last_group:
                self.finish_norm()

        g1(tasks[0])
        for i, task in enumerate(tasks):
            if i + 1 < len(tasks):
                g1(tasks[i + 1])
            g2(task)

    def place_dequantising(self):
        at = 0
        first = next(s for s in self.steps if s.kind == "G1")
        freed = max(i for i, s in enumerate(self.steps)
                    if s.kind == "D" and s.task.kind == CROSS1 and s.task.wset == self.last_cross - 1)
        per_set = 3 * (len(CODES_USED) + 1)
        for i, s in enumerate(self.steps):
            limit = per_set if i < freed else 2 * per_set if i < self.steps.index(first) else FSETS * per_set
            count = 0
            if s.kind == "D" and s.task.kind == CROSS1 and not (s.task.last_group and s.tiles[0]):
                count = 3 if s.task.last_set else 2 if s.tiles[0] == 0 else 4
            elif s.kind == "G1":
                count = 3
            elif s.kind == "G2":
                count = 8
            end = min(at + count, limit)
            s.pieces = (at, end)
            at = end
        assert at == FSETS * per_set


def decoder_kernel(nc, x_tok, x_T, ctx_T, pos, mask, hd_w, cross0_w, c1T, c2T, w1T, w2t, cross1_w,
                   gate_q, gate_s, up_q, up_s, down_q, down_s, consts, out):
    plan = Plan()
    steps = plan.steps
    units = plan.by_unit
    cross_tasks = [u.task for u in units if u.first]
    hd_units = plan.hd_units
    first_cross1 = next(u for u in units if u.task.kind == CROSS1)

    with ExitStack() as ctx:
        def sb(name, shape, dt=F32):
            return ctx.enter_context(nc.sbuf_tensor(name, shape, dt))

        def sem(name):
            return ctx.enter_context(nc.semaphore(name))

        X = sb("X", [P, TOK // P, DIM])
        HT = sb("HT", [P, KC, 2 * TOK])
        W = sb("W", [P, 2 * 5120])
        QT = sb("QT", [P, GB, 4, SEQ])
        OT = sb("OT", [P, 4, GT])
        PT = sb("PT", [P, 2, 1024])
        E = sb("E", [P, 4, 512])
        SW = sb("SW", [P, 2, 512])
        KR = sb("KR", [P, 1536])
        VR = sb("VR", [P, 2, 1024])
        AUX = sb("AUX", [P, 4096])
        VB = sb("VB", [P, 2, 512])
        ident = sb("ident", [P, P])
        causal = sb("causal", [P, SEQ])
        rope16 = sb("rope16", [P, 2, SEQ])
        small = sb("small", [P, 152])
        taken = [0]

        def part(*shape):
            n = int(np.prod(shape))
            ap = small[:, taken[0]:taken[0] + n]
            taken[0] += n
            return ap.rearrange("p (a b) -> p a b", a=shape[0]) if len(shape) == 2 else ap

        own_head = part(8)
        masked = part(1)
        mx, sums, rinv = part(4, 8), part(4, 8), part(4, 8)
        stats, meanvar = part(TILES, 6), part(TILES, 2)
        vareps, rstd, minus_half = part(TILES), part(TILES), part(TILES)

        KT = KR[:, 0:512]
        KT1 = KR[:, 0:1024]
        Kbd = KR[:, 512:1536].rearrange("p (r n) -> p r n", r=2)
        amask = KR[:, 512:1536].bitcast(U16)
        mask_raw = PT[:, :, :].rearrange("p a n -> p (a n)").bitcast(I32)
        cosT, sinT = AUX[:, 0:TOK], AUX[:, TOK:2 * TOK]
        posi = W[:, 5120:5120 + 2048].bitcast(I32)
        posf = W[:, 5120:5120 + 2048]
        onehot = W[:, 7168:8192].rearrange("p (r n) -> p r n", r=2)
        ptab = W[:, 8192:8192 + 512].rearrange("p (k n) -> p k n", k=4)
        iota = W[:, 9216:9220]
        QTf = QT[:, :, :, :].rearrange("p b a n -> p (b a n)")
        paired = HT[:, :, :].rearrange("p c (b e s) -> p c b e s", e=2, s=SEQ)
        OTf = OT[:, :, :].rearrange("p a n -> p (a n)")
        PTf = PT[:, :, :].rearrange("p a n -> p (a n)")
        Ef = E[:, :, :].rearrange("p a n -> p (a n)")
        SWf = SW[:, :, :].rearrange("p a n -> p (a n)")
        VBf = VB[:, :, :].rearrange("p a n -> p (a n)")
        zT = AUX[0:RANK, 0:TOK]
        chosen = QTf[:, 0:1024].bitcast(BF16).rearrange("p (r i n) -> p r i n", r=2, i=TILES)
        chosenT = QTf[:, 1024:1536].bitcast(BF16).rearrange("p (c n) -> p c n", c=2)
        relu = OTf.rearrange("p (r c n) -> p r c n", r=2, c=2)
        hsel = PTf[:, 0:1024].rearrange("p (c n) -> p c n", c=2)
        blkmax = sums
        ties = Ef[:, 0:64].bitcast(BF16)
        ties_f = SWf[:, 0:P]
        ident_b = Ef[:, 64:128].bitcast(BF16)
        c1_sb = Ef[:, 128:192].rearrange("p (c n) -> p c n", c=KC)
        c2_sb = Ef[0:RANK, 192:192 + INTER]
        silu = PTf.rearrange("p (r c n) -> p r c n", r=2, c=2)
        hgate = OTf.rearrange("p (r c n) -> p r c n", r=2, c=2)
        dq = [AUX[:, 0:3072], W[:, 5120:8192], W[:, 0:3072]]
        dq_q = SWf.bitcast(I32)
        dq_s = AUX[:, 3072:4096]
        dq_b = VBf[:, 0:512].bitcast(BF16)
        dq_e = VBf[:, 512:1024].bitcast(BF16)

        def x_cols(stage, c, group):
            if stage <= 3:
                return HT[:, c, TOK + group * GT:TOK + (group + 1) * GT]
            return paired[:, c, group * GB:(group + 1) * GB, 1, :]

        def wslot(wset):
            return W[:, 5120 * (wset % 2):5120 * (wset % 2) + 5120]

        def weights(kind, wset):
            w = wslot(wset)
            if kind == CROSS1:
                return (w[:, 0:1536].rearrange("p (c n) -> p c n", c=KC),
                        w[:, 1536:1920].rearrange("p (c n) -> p c n", c=KC),
                        w[:, 1920:2304].rearrange("p (c n) -> p c n", c=KC),
                        w[:, 2304:3840].rearrange("p (j n) -> p j n", j=3))
            return (w[:, 0:2048].rearrange("p (c n) -> p c n", c=KC),
                    w[:, 2048:2560].rearrange("p (c n) -> p c n", c=KC),
                    w[:, 2560:3072].rearrange("p (c n) -> p c n", c=KC),
                    w[:, 3072:5120].rearrange("p (j n) -> p j n", j=4))

        def ffn_weights(w):
            return (w[:, 0:1024].rearrange("p (c n) -> p c n", c=KC),
                    w[:, 1024:2048].rearrange("p (c n) -> p c n", c=2))

        def quarter_q(st):
            return QT[:, 2 * st.part:2 * st.part + 2, :, :].rearrange("p b j s -> p j b s")

        def quarter_k(st):
            return blocked(KT[:, st.part * P:(st.part + 1) * P], 2)

        def v_buf(task):
            return VR[:, task.n % 2, :]

        banks = {r: [ctx.enter_context(nc.psum_tensor(f"{r}{i}", [P, 512], F32)) for i in range(2)]
                 for r in ("pp", "sc", "tr", "ou")}

        def bank(ring, u):
            return banks[ring][u.n % 2]

        full = {r: sem(f"{r}_full") for r in banks}
        by_act = {r: sem(f"{r}_read_by_act") for r in banks}
        by_dve = {r: sem(f"{r}_read_by_dve") for r in banks}
        s_const = sem("consts_loaded")
        s_pos = sem("positions_loaded")
        s_ptab = sem("rope_table_loaded")
        s_x = sem("x_loaded")
        s_ht = [sem(f"xT_{g}_loaded") for g in range(GROUPS)]
        s_ctx = sem("ctxT_loaded")
        s_paired = [sem(f"paired_context_{g}_loaded") for g in range(GROUPS)]
        s_w = [sem("weights_even_loaded"), sem("weights_odd_loaded")]
        s_first_o = sem("first_output_weights_loaded")
        s_mraw = sem("mask_loaded")
        s_fc = sem("ffn0_consts_loaded")
        s_fcb = sem("ffn0_consts_in_bf16")
        s_init = sem("buffers_initialised")
        s_posf = sem("positions_ready")
        s_oh = sem("onehot_ready")
        s_ohused = sem("onehot_used")
        s_amask = sem("mask_ready")
        s_swap = sem("swapped_halves")
        s_swsin = sem("swapped_times_sin")
        s_rope = sem("rope_done")
        s_kbd = sem("kbd_ready")
        s_vbd = sem("vbd_ready")
        s_max = sem("row_max")
        s_pred = sem("mask_applied")
        s_sub = sem("max_subtracted")
        s_exp = sem("exp_done")
        s_sum = sem("row_sum")
        s_rinv = sem("row_sum_inverted")
        s_prob = sem("probs_ready")
        s_stat = sem("tile_stats")
        s_mv = sem("mean_var")
        s_ve = sem("var_plus_eps")
        s_rstd = sem("rstd_ready")
        s_xn = sem("x_normed")
        s_bmax = sem("block_max")
        s_chosen = sem("chosen_ready")
        s_dqq = sem("dq_codes_loaded")
        s_dqs = sem("dq_scales_loaded")
        s_dqb = sem("dq_codes_converted")
        s_dqe = sem("dq_equal")
        s_dqa = sem("dq_added")
        s_dqd = sem("dq_matrix_done")
        s_out = sem("out_stored")

        block = ctx.enter_context(nc.Block())

        def set_kind(w):
            for stage, kind, sets in STAGES:
                if w < sets:
                    return stage, kind, w
                w -= sets
            return None

        dma_count = [0, 0]
        loaded = {}
        n_sets = sum(s for _, k, s in STAGES if k != "ffn1")
        for w in range(n_sets):
            _, kind, _ = set_kind(w)
            dma_count[w % 2] += 16 * (2 if kind == "ffn0" else 4 if w else 3)
            loaded[w] = dma_count[w % 2]

        stage3 = [t for t in cross_tasks if t.stage == 3]
        ffn_tasks = [st.task for st in steps if st.kind == "F1"]
        gate_tasks = [st.task for st in steps if st.kind == "G1"]
        cross0_first = next(t.n for t in cross_tasks if t.kind == CROSS0)

        def blocked(ap, n):
            return ap.rearrange("p (g k) -> p g k", g=n)

        def read(eng, ring, *uses):
            for u in uses:
                if u.act is not None:
                    eng.wait_ge(by_act[ring], u.act)
                if u.dve is not None:
                    eng.wait_ge(by_dve[ring], u.dve)

        def before(task):
            return cross_tasks[task.n - 1]

        def values_free(eng, task):
            if task.n >= 2:
                old = cross_tasks[task.n - 2]
                if old.kind == HD16:
                    eng.wait_ge(s_vbd, old.last_kbd + 1)
                else:
                    eng.wait_ge(full["ou"], old.units[-1].ou[-1].n + 1)

        per_matrix = len(CODES_USED) + 1

        @block.sync
        def _(sp):
            sp.dma_start(posi, pos.to_broadcast([P, TOK])).then_inc(s_pos, 16)
            for dst, name in ((ident[:, :], "ident"), (causal[:, :], "causal"), (own_head, "own_head"), (iota, "iota")):
                sp.dma_start(dst, consts[name]).then_inc(s_const, 16)
            sp.dma_start(rope16[:, :, :], consts["rope16"]).then_inc(s_const, 16)

            def load_set(w):
                stage, kind, sub = set_kind(w)
                s = s_w[w % 2]
                dst = W[:, 5120 * (w % 2):5120 * (w % 2) + 5120]
                if kind == "ffn0":
                    a, b = ffn_weights(dst)
                    sp.dma_start(a, w1T[:, sub * ROW:(sub + 1) * ROW].rearrange("(c p) n -> p c n", p=P)).then_inc(s, 16)
                    sp.dma_start(b, w2t[sub * ROW:(sub + 1) * ROW, :].rearrange("(c p) n -> p c n", p=P)).then_inc(s, 16)
                    return
                q, k, v, o = weights(kind, w)
                if kind == HD16:
                    dq_, dk, dv, do = hd_w[0 if stage == 0 else 1]
                    width, head = 512, P
                elif kind == CROSS0:
                    dq_, dk, dv, do = cross0_w
                    width, head = 512, P
                else:
                    dq_, dk, dv, do = cross1_w
                    width, head = 384, 96
                sp.dma_start(q, dq_[:, sub * width:(sub + 1) * width].rearrange("(c p) n -> p c n", p=P)).then_inc(s, 16)
                sp.dma_start(k, dk[:, sub * head:(sub + 1) * head].rearrange("(c p) n -> p c n", p=P)).then_inc(s, 16)
                sp.dma_start(v, dv[:, sub * head:(sub + 1) * head].rearrange("(c p) n -> p c n", p=P)).then_inc(s, 16)
                if w:
                    sp.dma_start(o, do[sub * width:(sub + 1) * width, :].rearrange("(j p) n -> p j n", p=P)).then_inc(s, 16)

            def load_codes(m):
                s, which = divmod(m, 3)
                if m:
                    sp.wait_ge(s_dqb, m)
                else:
                    sp.wait_ge(s_rope, plan.ropes)
                    sp.wait_ge(full["ou"], plan.hd_units[-1].task.d[-1].n + 1)
                q = (gate_q, up_q, down_q)[which]
                if which < 2:
                    dst = dq_q.rearrange("p (c n) -> p c n", c=KC)
                    src = q[:, s * ROW:(s + 1) * ROW].rearrange("(c p) n -> p c n", p=P)
                else:
                    dst = dq_q.rearrange("p (c n) -> p c n", c=2)
                    src = q[s * ROW:(s + 1) * ROW, :].rearrange("(c p) n -> p c n", p=P)
                sp.dma_start(dst, src).then_inc(s_dqq, 16)

            def load_scales(m):
                s, which = divmod(m, 3)
                if m:
                    sp.wait_ge(s_dqd, m)
                for half in range(2):
                    if which < 2:
                        sc = (gate_s, up_s)[which].rearrange("(c h) n -> h c n", h=2)[half, :, s * ROW:(s + 1) * ROW]
                        dst = dq_s[64 * half:64 * half + 64, :].rearrange("p (c n) -> p c n", c=KC)
                        shape = [64, KC, ROW]
                    else:
                        sc = down_s[4 * s:4 * s + 4, :].rearrange("(c h) n -> h c n", h=2)[half, :, :]
                        dst = dq_s[64 * half:64 * half + 64, :].rearrange("p (c n) -> p c n", c=2)
                        shape = [64, 2, DIM]
                    sp.dma_start(dst, sc.unsqueeze(0).to_broadcast(shape)).then_inc(s_dqs, 16)

            def load_paired(group):
                for c in range(KC):
                    src = ctx_T[c * P:(c + 1) * P, group * GT:(group + 1) * GT]
                    sp.dma_start(paired[:, c, group * GB:(group + 1) * GB, 0, :],
                                 src.rearrange("p (b s) -> p b s", s=SEQ)).then_inc(s_paired[group], 16)

            load_set(0)
            for g in range(GROUPS):
                if g == 1:
                    sp.dma_start(ptab, consts["ptab"].rearrange("(k p) n -> p k n", p=P)).then_inc(s_ptab, 16)
                    sp.dma_start(weights(HD16, 0)[3],
                                 hd_w[0][3].rearrange("(j p) n -> p j n", p=P)).then_inc(s_first_o, 16)
                sp.dma_start(HT[:, :, TOK + g * GT:TOK + (g + 1) * GT],
                             x_T[:, g * GT:(g + 1) * GT].rearrange("(c p) n -> p c n", p=P)).then_inc(s_ht[g], 16)
            for t in range(GROUPS):
                sp.dma_start(X[:, t * TILES:(t + 1) * TILES, :],
                             x_tok[t * GT:(t + 1) * GT, :].rearrange("(n p) d -> p n d", p=P)).then_inc(s_x, 16)
            for c in range(KC):
                sp.dma_start(HT[:, c, 0:TOK], ctx_T[c * P:(c + 1) * P, :]).then_inc(s_ctx, 16)
            for st in steps:
                if st.kind == "POS" and st.group == GROUPS - 1:
                    sp.wait_ge(full["pp"], st.pp[0].n + 1)
                    sp.wait_ge(s_oh, 4 * GROUPS)
                    load_set(1)
                if st.kind == "FC":
                    sp.wait_ge(full["pp"], st.pp_before)
                    load_paired(0)
                    load_paired(1)
                if st.kind == "LN" and st.stage == 3 and st.group in (1, 3):
                    sp.wait_ge(full["pp"], stage3[st.group].quarters[-1].kv.n + 1)
                    load_paired(2 + st.group // 2)
                if st.kind == "MASK":
                    sp.wait_ge(full["ou"], st.ou_before)
                    src = mask.rearrange("b q k -> q b k")
                    raw = mask_raw.rearrange("p (b k) -> p b k", k=SEQ)
                    for half in range(2):
                        sp.dma_start(raw[64 * half:64 * half + 64], src).then_inc(s_mraw, 16)
                if st.kind == "FC":
                    sp.wait_ge(full["tr"], st.tr_before)
                    sp.wait_ge(s_rope, st.ropes_before)
                    sp.dma_start(ties_f, consts["ties"]).then_inc(s_fc, 16)
                    sp.dma_start(c1_sb, c1T.rearrange("(c p) n -> p c n", p=P)).then_inc(s_fc, 16)
                    sp.dma_start(c2_sb, c2T).then_inc(s_fc, 16)
                done = None
                if (st.kind == "F4" or st.kind == "D" and TILES - 1 in st.tiles) and st.task.group == GROUPS - 1:
                    done = st.task.wset
                if done is not None and done + 2 < n_sets:
                    sp.wait_ge(full["ou"], plan.set_done[done])
                    load_set(done + 2)
                for p in range(*st.pieces):
                    m, k = divmod(p, per_matrix)
                    if k == 1 and m + 1 < 3 * FSETS:
                        load_codes(m + 1)
                    if k == per_matrix - 1 and m + 1 < 3 * FSETS:
                        load_scales(m + 1)
                if st.kind == "B" and st.unit is first_cross1:
                    load_codes(0)
                    load_scales(0)
                if st.kind == "LN" and st.final:
                    sp.wait_ge(s_xn, TILES * (st.n + 1))
                    g = st.group
                    sp.dma_start(out[g * GT:(g + 1) * GT, :].rearrange("(n p) d -> p n d", p=P),
                                 X[:, g * TILES:(g + 1) * TILES, :]).then_inc(s_out, 16)
            sp.wait_ge(s_out, 16 * GROUPS)

        @block.gpsimd
        def _(pool):
            pool.memset(VB[:, :, :], 0.0).then_inc(s_init, 1)
            pool.memset(masked, MASKED).then_inc(s_init, 1)
            pool.memset(minus_half, -0.5).then_inc(s_init, 1)
            pool.wait_ge(s_init, 3)
            pool.wait_ge(s_const, 5 * 16)

            def make_kbd(unit):
                r = unit.kbd
                pool.wait_ge(s_rope, unit.rope_done)
                if r >= 2:
                    pool.wait_ge(full["sc"], hd_units[r - 2].b.sc[1].n + 1)
                if st.kind == "AQ" and st.task.stage == 3:
                    pool.wait_ge(full["sc"], st.sc_before)
                    pool.wait_ge(by_dve["sc"], plan.rings["sc"][st.sc_before - 1].dve)
                b = unit.i
                pool.tensor_tensor(Kbd[:, r % 2, :].rearrange("p (g k) -> p g k", g=8),
                                   KT[:, b * SEQ:(b + 1) * SEQ].unsqueeze(1).to_broadcast([P, 8, SEQ]),
                                   own_head.unsqueeze(2).to_broadcast([P, 8, SEQ]),
                                   ALU.mult).then_inc(s_kbd, 1)

            for st in steps:
                for p in range(*st.pieces):
                    m, k = divmod(p, per_matrix)
                    if k == per_matrix - 1:
                        s, which = divmod(m, 3)
                        acc = dq[s % 3][:, 1024 * which:1024 * which + 1024]
                        pool.wait_ge(s_dqe, (m + 1) * (2 * len(CODES_USED) - 1))
                        pool.wait_ge(s_dqs, 32 * (m + 1))
                        pool.tensor_tensor(acc, acc, dq_s, ALU.mult).then_inc(s_dqd, 1)
                if st.kind == "A" and st.task.kind == CROSS0:
                    sinv = blocked(sinT[:, st.task.group * GT:(st.task.group + 1) * GT], GB)
                    for what, i, u, r in st.items:
                        if r is None:
                            continue
                        pool.wait_ge(by_act["pp"], u.act)
                        sw3 = blocked(SW[:, r % 2, :], GB)
                        pool.tensor_tensor(sw3, sw3, sinv, ALU.mult).then_inc(s_swsin, 1)
                        dst = QT[:, :, i, :] if what == "q" else blocked(KT, GB)
                        pool.wait_ge(s_swsin, r + 1)
                        pool.wait_ge(by_dve["pp"], u.dve)
                        pool.tensor_tensor(dst, dst, sw3, ALU.add).then_inc(s_rope, 1)
                if st.kind == "AQ":
                    for r, u, n, dst in ((st.rope, st.q, 8, quarter_q(st)), (st.rope + 1, st.kv, 2, quarter_k(st))):
                        pool.wait_ge(by_act["pp"], u.act)
                        sw3 = blocked(SW[:, r % 2, 0:n * SEQ], n)
                        pool.tensor_tensor(sw3, sw3, rope16[:, 1, :].unsqueeze(1).to_broadcast([P, n, SEQ]),
                                           ALU.mult).then_inc(s_swsin, 1)
                        pool.wait_ge(s_swsin, r + 1)
                        pool.wait_ge(by_dve["pp"], u.dve)
                        if n == 8:
                            sw3 = SW[:, r % 2, :].rearrange("p (j b s) -> p j b s", j=4, b=2)
                        pool.tensor_tensor(dst, dst, sw3, ALU.add).then_inc(s_rope, 1)
                    if st.task.first and st.part == 0:
                        make_kbd(st.task.units[0])
                if st.kind == "B":
                    unit = st.unit
                    if unit.task.kind == HD16:
                        if units[unit.n + 1].task.kind == HD16:
                            make_kbd(units[unit.n + 1])
                    blocks = 4 if unit.task.kind == CROSS1 else 8
                    for i in range(2):
                        n = 2 * unit.n + i
                        e3 = E[:, n % 4, :].rearrange("p (g k) -> p g k", g=blocks)
                        pool.wait_ge(s_rinv, n + 1)
                        pool.tensor_tensor(e3, e3, rinv[:, n % 4, 0:blocks].unsqueeze(2).to_broadcast([P, blocks, 512 // blocks]),
                                           ALU.mult).then_inc(s_prob, 1)
                if st.kind == "LS":
                    pool.wait_ge(s_mv, st.n + 1)
                    pool.tensor_scalar(vareps, meanvar[:, :, 1], EPS, None, ALU.add).then_inc(s_ve, 1)
                    pool.wait_ge(s_ve, st.n + 1)
                    pool.tensor_tensor(rstd, vareps, minus_half, ALU.pow).then_inc(s_rstd, 1)

        @block.scalar
        def _(act):
            def make_vbd(unit):
                r = unit.kbd
                read(act, "pp", unit.quarter.kv)
                if r >= 2:
                    act.wait_ge(full["ou"], hd_units[r - 2].ou[0].n + 1)
                src = v_buf(unit.task).rearrange("p (b g e d) -> p b g e d", b=GB, g=4, e=2)
                for half in range(2):
                    rows = slice(64 * half, 64 * half + 64)
                    row = VB[rows, r % 2, :]
                    dst = bass.AP(row.tensor, row.offset + 16 * half, [list(row.ap[0]), [2 * 16 + P, 4], [1, 16]])
                    ins = act.activation(dst, src[rows, unit.i, :, half, :], ACT.Copy)
                ins.then_inc(s_vbd, 1)

            def swap_halves(r, u, n):
                if r >= 2:
                    act.wait_ge(s_rope, r - 1)
                act.activation(SW[0:64, r % 2, 0:n], bank("pp", u)[64:P, 0:n], ACT.Copy)
                return act.activation(SW[64:P, r % 2, 0:n], bank("pp", u)[0:64, 0:n], ACT.Copy)

            def exponential(unit, i):
                n = 2 * unit.n + i
                if unit.task.kind == HD16:
                    act.wait_ge(s_sub, 2 * unit.kbd + i + 1)
                else:
                    act.wait_ge(by_dve["sc"], unit.b.sc[i].dve)
                act.activation(E[:, n % 4, :], E[:, n % 4, :], ACT.Exp,
                               scale=SCALE[unit.task.kind]).then_inc(s_exp, 1)

            act.wait_ge(s_init, 3)
            late = None
            for st in steps:
                if st.kind == "POS":
                    u = st.pp[0]
                    cols = slice(st.group * GT, (st.group + 1) * GT)
                    act.wait_ge(full["pp"], u.n + 1)
                    act.activation(cosT[0:64, cols], bank("pp", u)[0:64, :], ACT.Copy)
                    act.activation(cosT[64:P, cols], bank("pp", u)[0:64, :], ACT.Copy).then_inc(by_act["pp"], 1)
                if st.kind == "Z":
                    u = st.pp[0]
                    act.wait_ge(full["pp"], u.n + 1)
                    act.activation(zT[:, st.group * GT:(st.group + 1) * GT], bank("pp", u)[0:RANK, :],
                                   ACT.Copy).then_inc(by_act["pp"], 1)
                if st.kind == "A":
                    task = st.task
                    if task.kind == CROSS1 and st.part == 0:
                        act.wait_ge(full["sc"], st.sc_before)
                        act.wait_ge(s_kbd, st.kbd_before)
                    v = v_buf(task)
                    for what, i, u, r in st.items:
                        if u.act is None:
                            continue
                        act.wait_ge(full["pp"], u.n + 1)
                        ps = bank("pp", u)
                        if r is not None:
                            swap_halves(r, u, 512).then_inc(by_act["pp"], 1)
                        elif what == "v":
                            values_free(act, task)
                            n = 512 if task.kind == CROSS0 else 384
                            act.activation(v[:, i * 384:i * 384 + n], ps[:, 0:n], ACT.Copy).then_inc(by_act["pp"], 1)
                        elif what == "q":
                            act.activation(QT[0:96, :, i, :], blocked(ps[0:96, :], GB), ACT.Copy)
                            act.activation(QT[32 * i:32 * i + 32, :, 3, :], blocked(ps[96:P, :], GB),
                                           ACT.Copy).then_inc(by_act["pp"], 1)
                        else:
                            act.activation(KT1[0:96, i * 512:(i + 1) * 512], ps[0:96, :],
                                           ACT.Copy).then_inc(by_act["pp"], 1)
                if st.kind == "AQ":
                    act.wait_ge(full["pp"], st.q.n + 1)
                    swap_halves(st.rope, st.q, 512).then_inc(by_act["pp"], 1)
                    act.wait_ge(full["pp"], st.kv.n + 1)
                    swap_halves(st.rope + 1, st.kv, P)
                    values_free(act, st.task)
                    v2 = v_buf(st.task)[:, st.part * 256:(st.part + 1) * 256].rearrange("p (e f) -> p e f", e=2)
                    ps = bank("pp", st.kv)
                    act.activation(v2[0:64, 0, :], ps[0:64, P:2 * P], ACT.Copy)
                    act.activation(v2[64:P, 1, :], ps[64:P, P:2 * P], ACT.Copy).then_inc(by_act["pp"], 1)
                if st.kind == "B":
                    unit = st.unit
                    if unit.task.kind == HD16:
                        make_vbd(unit)
                    exponential(unit, 0)
                    if unit.exp_late:
                        late = unit
                    else:
                        exponential(unit, 1)
                if st.kind == "T":
                    unit = st.unit
                    if unit.n >= 2:
                        act.wait_ge(full["ou"], units[unit.n - 2].ou[-1].n + 1)
                    if unit.task.kind == CROSS0:
                        act.wait_ge(s_amask, 1)
                    for i, u in enumerate(st.tr):
                        act.wait_ge(full["tr"], u.n + 1)
                        if unit.task.kind == CROSS1:
                            dst = PT[:, unit.n % 2, i * 512:(i + 1) * 512]
                            src = bank("tr", u)[:, :]
                        else:
                            dst = PT[:, unit.n % 2, :].rearrange("p (b h q) -> p b h q", b=4, h=2)[:, :, i, :]
                            src = bank("tr", u)[:, :].rearrange("p (b q) -> p b q", b=4)
                        act.activation(dst, src, ACT.Copy).then_inc(by_act["tr"], 1)
                        if late:
                            exponential(late, 1)
                            late = None
                if st.kind == "C":
                    unit = st.unit
                    task = unit.task
                    if unit.first and task.n and st.part == 0 and before(task).kind != HD16:
                        act.wait_ge(full["ou"], before(task).d[-1].n + 1)
                    elif task.n and st.part == 0 and before(task).kind == HD16:
                        last = (unit.i + 1) * TILES // len(task.units) - 1 if task.kind != HD16 else unit.i // 2
                        act.wait_ge(full["ou"], before(task).d[last].n + 1)
                    for i, u in enumerate(st.ou):
                        act.wait_ge(full["ou"], u.n + 1)
                        ps = bank("ou", u)
                        if task.kind == HD16:
                            dst = OT[:, :, unit.i * SEQ:(unit.i + 1) * SEQ]
                            src = ps[:, 0:256].rearrange("p (h q) -> p h q", h=4)
                        elif task.kind == CROSS0:
                            m = st.part
                            dst = OT[:, :, 256 * m:256 * m + 256].rearrange(
                                "p h (x e q) -> p e x h q", x=2, e=2)[:, i]
                            src = ps[:, :].rearrange("p (x h q) -> p x h q", x=2, h=4)
                        else:
                            b = 4 * unit.i + 2 * i
                            cols = slice(b * SEQ, (b + 2) * SEQ)
                            src = ps[0:96, :].rearrange("p (b h q) -> p b h q", b=2, h=4)
                            for k in range(3):
                                act.activation(blocked(OT[96:P, k, cols], 2), src[32 * k:32 * k + 32, :, 3, :], ACT.Copy)
                            dst = OT[0:96, 0:3, cols].rearrange("p h (b q) -> p b h q", b=2)
                            src = src[:, :, 0:3, :]
                        act.activation(dst, src, ACT.Copy).then_inc(by_act["ou"], 1)
                if st.kind == "LNT":
                    for i, u in enumerate(st.tr):
                        act.wait_ge(full["tr"], u.n + 1)
                        b = st.group * GB + 2 * i
                        if st.stage < 3:
                            dst = HT[:, :, TOK + b * SEQ:TOK + (b + 2) * SEQ]
                            src = bank("tr", u)[:, :].rearrange("p (c n) -> p c n", c=KC)
                        else:
                            dst = paired[:, :, b:b + 2, 1, :]
                            src = bank("tr", u)[:, :].rearrange("p (c b s) -> p c b s", c=KC, b=2)
                        act.activation(dst, src, ACT.Copy).then_inc(by_act["tr"], 1)
                if st.kind == "F1":
                    task = st.task
                    if task.n >= 2:
                        act.wait_ge(by_dve["sc"], ffn_tasks[task.n - 2].f3.sc[1].dve)
                    act.wait_ge(full["pp"], st.pp[0].n + 1)
                    act.activation(relu[:, task.n % 2, 0, :], bank("pp", st.pp[0])[:, :],
                                   ACT.Relu).then_inc(by_act["pp"], 1)
                if st.kind == "F2":
                    task = st.task
                    if task.n:
                        act.wait_ge(full["sc"], ffn_tasks[task.n - 1].f3.sc[1].n + 1)
                    for c, u in enumerate(st.tr):
                        act.wait_ge(full["tr"], u.n + 1)
                        act.activation(chosenT[:, c, :], bank("tr", u)[:, 0:256].bitcast(BF16),
                                       ACT.Copy).then_inc(by_act["tr"], 1)
                if st.kind == "G1":
                    task = st.task
                    if task.n >= 2:
                        act.wait_ge(by_dve["sc"], gate_tasks[task.n - 2].g1.up[1].dve)
                    for c, u in enumerate(st.gate):
                        act.wait_ge(full["pp"], u.n + 1)
                        act.activation(silu[:, task.n % 2, c, :], bank("pp", u)[:, :],
                                       ACT.Silu).then_inc(by_act["pp"], 1)

        @block.vector
        def _(dve):
            def then_wait(ins, s, n):
                ins.then_inc(s, 1)
                dve.wait_ge(s, n)

            dve.wait_ge(s_pos, 16)
            wrap = onehot.rearrange("p r n -> p (r n)")
            for i in range(2):
                part = slice(i * 1024, (i + 1) * 1024)
                then_wait(dve.tensor_scalar(wrap, posi[:, part], 0.0, float(POSITIONS), ALU.is_lt, ALU.mult), s_posf, 3 * i + 1)
                then_wait(dve.tensor_tensor(posf[:, part], posi[:, part], wrap, ALU.add), s_posf, 3 * i + 2)
                then_wait(dve.tensor_scalar(posf[:, part], posf[:, part], 0.0, POSITIONS - 1.0, ALU.max, ALU.min), s_posf, 3 * i + 3)
            dve.wait_ge(s_const, 5 * 16)
            dve.wait_ge(s_init, 3)
            chain = [0]

            def dequantise(p):
                m, k = divmod(p, per_matrix)
                s, which = divmod(m, 3)
                acc = dq[s % 3][:, 1024 * which:1024 * which + 1024]

                def link(ins):
                    chain[0] += 1
                    ins.then_inc(s_dqe, 1)

                if chain[0]:
                    dve.wait_ge(s_dqe, chain[0])
                if k == 0:
                    dve.wait_ge(s_dqq, 16 * (m + 1))
                    dve.tensor_copy(dq_b, dq_q).then_inc(s_dqb, 1)
                    return
                code = CODES_USED[k - 1]
                if k == 1:
                    dve.wait_ge(s_dqb, m + 1)
                    if s >= 3:
                        if which < 2:
                            g1 = gate_tasks[GROUPS * (s - 2) - 1].g1
                            dve.wait_ge(full["pp"], g1.gate[1].n + 1)
                            dve.wait_ge(full["sc"], g1.up[1].n + 1)
                        else:
                            dve.wait_ge(full["ou"], gate_tasks[GROUPS * (s - 2) - 1].g2.ou[-1].n + 1)
                    elif s:
                        dve.wait_ge(full["ou"], plan.set_done[n_sets - 3 + s])
                    link(dve.tensor_scalar(acc, dq_b, float(code), float(CODE[code]), ALU.is_equal, ALU.mult))
                    return
                link(dve.tensor_scalar(dq_e, dq_b, float(code), None, ALU.is_equal))
                dve.wait_ge(s_dqe, chain[0])
                link(dve.scalar_tensor_tensor(out=acc, in0=dq_e, scalar=float(CODE[code]), in1=acc,
                                              op0=ALU.mult, op1=ALU.add))

            def pieces(st, a, b):
                for p in range(st.pieces[0] + a, min(st.pieces[0] + b, st.pieces[1])):
                    dequantise(p)

            for st in steps:
                if st.kind == "POS":
                    for k in range(4):
                        n = 4 * st.group + k
                        if n >= 2:
                            g, j = divmod(n - 2, 4)
                            if j < 3:
                                dve.wait_ge(s_ohused, 3 * g + j + 1)
                            else:
                                dve.wait_ge(full["pp"], plan.pos_steps[g].pp[0].n + 1)
                        dve.tensor_scalar(onehot[:, n % 2, :], posf[:, st.group * GT:(st.group + 1) * GT],
                                          iota[:, k:k + 1], None, ALU.is_equal).then_inc(s_oh, 1)
                    u = st.pp[0]
                    cols = slice(st.group * GT, (st.group + 1) * GT)
                    dve.wait_ge(full["pp"], u.n + 1)
                    dve.tensor_scalar(sinT[0:64, cols], bank("pp", u)[64:P, :], -1.0, None, ALU.mult)
                    dve.tensor_copy(sinT[64:P, cols], bank("pp", u)[64:P, :]).then_inc(by_dve["pp"], 1)
                if st.kind == "FC":
                    dve.wait_ge(full["tr"], st.tr_before)
                    dve.tensor_copy(ident_b, ident[:, :]).then_inc(s_fcb, 1)
                    dve.wait_ge(s_fc, 48)
                    dve.tensor_copy(ties, ties_f).then_inc(s_fcb, 1)
                if st.kind == "MASK":
                    dve.wait_ge(s_mraw, 32)
                    dve.wait_ge(full["sc"], st.sc_before)
                    dve.tensor_scalar(amask, mask_raw, 0.0, None, ALU.is_equal).then_inc(s_amask, 1)
                if st.kind == "A" and st.part == 0 or st.kind == "AQ":
                    dve.wait_ge(full["sc"], st.sc_before) if st.sc_before else None
                    dve.wait_ge(full["tr"], st.tr_before) if st.tr_before else None
                    dve.wait_ge(s_kbd, st.kbd_before) if st.kbd_before else None
                if st.kind == "A":
                    task = st.task
                    cosv = blocked(cosT[:, task.group * GT:(task.group + 1) * GT], GB)
                    if task.kind == CROSS0 and task.first:
                        dve.wait_ge(by_act["pp"], plan.pos_steps[-1].pp[0].act)
                    v = v_buf(task)
                    for what, i, u, r in st.items:
                        if u.dve is None:
                            continue
                        ps = bank("pp", u)
                        if r is not None:
                            dve.wait_ge(by_act["pp"], u.act)
                            dst = QT[:, :, i, :] if what == "q" else blocked(KT, GB)
                            dve.tensor_tensor(dst, blocked(ps[:, :], GB), cosv, ALU.mult).then_inc(by_dve["pp"], 1)
                            continue
                        dve.wait_ge(full["pp"], u.n + 1)
                        if what == "v":
                            values_free(dve, task)
                            dve.tensor_copy(v[:, i * 384:(i + 1) * 384], ps[:, 0:384]).then_inc(by_dve["pp"], 1)
                        elif what == "q":
                            dve.tensor_copy(QT[0:96, :, i, :], blocked(ps[0:96, :], GB))
                            dve.tensor_copy(QT[32 * i:32 * i + 32, :, 3, :],
                                            blocked(ps[96:P, :], GB)).then_inc(by_dve["pp"], 1)
                        else:
                            dve.tensor_copy(KT1[0:96, i * 512:(i + 1) * 512], ps[0:96, :]).then_inc(by_dve["pp"], 1)
                if st.kind == "AQ":
                    cos16 = rope16[:, 0, :].unsqueeze(1)
                    ps = bank("pp", st.q)
                    dve.wait_ge(by_act["pp"], st.q.act)
                    for j in range(4):
                        ins = dve.tensor_tensor(quarter_q(st)[:, j], blocked(ps[:, j * P:(j + 1) * P], 2),
                                                cos16.to_broadcast([P, 2, SEQ]), ALU.mult)
                    ins.then_inc(by_dve["pp"], 1)
                    ps = bank("pp", st.kv)
                    dve.wait_ge(by_act["pp"], st.kv.act)
                    dve.tensor_tensor(quarter_k(st), blocked(ps[:, 0:P], 2),
                                      cos16.to_broadcast([P, 2, SEQ]), ALU.mult)
                    values_free(dve, st.task)
                    v2 = v_buf(st.task)[:, st.part * 256:(st.part + 1) * 256].rearrange("p (e f) -> p e f", e=2)
                    dve.tensor_copy(v2[0:64, 1, :], ps[64:P, P:2 * P])
                    dve.tensor_copy(v2[64:P, 0, :], ps[0:64, P:2 * P]).then_inc(by_dve["pp"], 1)
                if st.kind == "B":
                    unit = st.unit
                    kind = unit.task.kind
                    blocks = 4 if kind == CROSS1 else 8

                    def head(i):
                        n = 2 * unit.n + i
                        u = st.sc[i]
                        ps = bank("sc", u)
                        e = E[:, n % 4, :]
                        dve.wait_ge(full["sc"], u.n + 1)
                        if unit.n >= 2:
                            dve.wait_ge(full["tr"], units[unit.n - 2].t.tr[i].n + 1)
                        if kind == HD16:
                            dve.tensor_tensor(blocked(e, 8), blocked(ps[:, :], 8),
                                              causal[:, :].unsqueeze(1).to_broadcast([P, 8, SEQ]),
                                              ALU.add).then_inc(by_dve["sc"], 1)
                            dve.wait_ge(by_dve["sc"], u.dve)
                            dve.tensor_reduce(mx[:, n % 4, :], blocked(e, 8), AX.X, ALU.max).then_inc(s_max, 1)
                            dve.wait_ge(s_max, n + 1)
                            dve.tensor_tensor(blocked(e, 8), blocked(e, 8),
                                              mx[:, n % 4, :].unsqueeze(2).to_broadcast([P, 8, SEQ]),
                                              ALU.subtract).then_inc(s_sub, 1)
                            return
                        if kind == CROSS0:
                            if unit.task.first and i == 0:
                                dve.wait_ge(s_amask, 1)
                            g = unit.task.group
                            dve.copy_predicated(ps[:, :], amask[:, g * GT:(g + 1) * GT],
                                                masked[:, 0:1].to_broadcast([P, 512])).then_inc(s_pred, 1)
                            dve.wait_ge(s_pred, 2 * (unit.task.n - cross0_first) + i + 1)
                        dve.tensor_reduce(mx[:, n % 4, 0:blocks], blocked(ps[:, :], blocks), AX.X, ALU.max).then_inc(s_max, 1)
                        dve.wait_ge(s_max, n + 1)
                        dve.tensor_tensor(blocked(e, blocks), blocked(ps[:, :], blocks),
                                          mx[:, n % 4, 0:blocks].unsqueeze(2).to_broadcast([P, blocks, 512 // blocks]),
                                          ALU.subtract).then_inc(by_dve["sc"], 1)

                    def tail(i):
                        n = 2 * unit.n + i
                        dve.wait_ge(s_exp, n + 1)
                        dve.tensor_reduce(sums[:, n % 4, 0:blocks], blocked(E[:, n % 4, :], blocks), AX.X,
                                          ALU.add).then_inc(s_sum, 1)
                        dve.wait_ge(s_sum, n + 1)
                        dve.reciprocal(rinv[:, n % 4, 0:blocks], sums[:, n % 4, 0:blocks]).then_inc(s_rinv, 1)

                    head(0)
                    head(1)
                    tail(0)
                    tail(1)
                if st.kind in ("D", "F4", "G2"):
                    task = st.task
                    if task.stage == 0:
                        dve.wait_ge(s_x, 16 * GROUPS)
                    if st.ou[0].dve > 1:
                        dve.wait_ge(by_dve["ou"], st.ou[0].dve - 1)
                    if task.first and task.stage:
                        dve.wait_ge(s_xn, TILES * GROUPS * task.stage - TILES * (GROUPS - 1))
                    for i, u in enumerate(st.ou):
                        tile = task.group * TILES + (st.tiles[i] if st.kind == "D" else i)
                        dve.wait_ge(full["ou"], u.n + 1)
                        dve.tensor_tensor(X[:, tile, :], X[:, tile, :], bank("ou", u)[:, :],
                                          ALU.add).then_inc(by_dve["ou"], 1)
                        if st.kind == "G2":
                            pieces(st, i, i + 1 if i < 3 else 8)
                    if st.kind == "D":
                        pieces(st, 0, 5)
                if st.kind == "LS":
                    dve.wait_ge(by_dve["ou"], st.added)
                    if st.n:
                        dve.wait_ge(s_xn, TILES * st.n)
                    for i in range(TILES):
                        dve.bn_stats(stats[:, i, :], X[:, st.group * TILES + i, :]).then_inc(s_stat, 1)
                    for i in range(TILES):
                        dve.wait_ge(s_stat, TILES * st.n + i + 1)
                        ins = dve.bn_aggr(meanvar[:, i, :], stats[:, i, :])
                    ins.then_inc(s_mv, 1)
                if st.kind == "LN":
                    dve.wait_ge(s_mv, st.n + 1)
                    dve.wait_ge(s_rstd, st.n + 1)
                    for i in range(TILES):
                        tile = st.group * TILES + i
                        dve.tensor_scalar(X[:, tile, :], X[:, tile, :], meanvar[:, i, 0:1], rstd[:, i:i + 1],
                                          ALU.subtract, ALU.mult).then_inc(s_xn, 1)
                if st.kind == "F1":
                    task = st.task
                    for i2, u in enumerate(st.sc):
                        n = 2 * task.n + i2
                        dve.wait_ge(full["sc"], u.n + 1)
                        ps = blocked(bank("sc", u)[:, :], 16)
                        mxb = blkmax[:, 2 * (n % 2):2 * (n % 2) + 2, :].rearrange("p a b -> p (a b)")
                        dve.tensor_reduce(mxb, ps, AX.X, ALU.max).then_inc(s_bmax, 1)
                        dve.wait_ge(s_bmax, n + 1)
                        if task.n >= 2:
                            dve.wait_ge(full["tr"], ffn_tasks[task.n - 2].f2.tr[1].n + 1)
                        dst = chosen[:, task.n % 2, 2 * i2:2 * i2 + 2, :].rearrange("p i (g k) -> p (i g) k", k=BLK)
                        dve.tensor_tensor(dst, ps, mxb.unsqueeze(2).to_broadcast([P, 16, BLK]),
                                          ALU.is_ge).then_inc(by_dve["sc"], 1)
                    if task.n >= 2:
                        dve.wait_ge(by_dve["sc"], ffn_tasks[task.n - 2].f3.sc[1].dve)
                    dve.wait_ge(full["pp"], st.pp[1].n + 1)
                    dve.tensor_scalar(relu[:, task.n % 2, 1, :], bank("pp", st.pp[1])[:, :], 0.0, None,
                                      ALU.max).then_inc(by_dve["pp"], 1)
                if st.kind == "F3":
                    task = st.task
                    read(dve, "pp", *task.f1.pp)
                    if task.n:
                        dve.wait_ge(full["ou"], ffn_tasks[task.n - 1].f4.ou[-1].n + 1)
                    for c, u in enumerate(st.sc):
                        dve.wait_ge(full["sc"], u.n + 1)
                        dve.scalar_tensor_tensor(out=hsel[:, c, :], in0=bank("sc", u)[:, :], scalar=-TIE,
                                                 in1=relu[:, task.n % 2, c, :], op0=ALU.is_equal,
                                                 op1=ALU.mult).then_inc(by_dve["sc"], 1)
                if st.kind == "G1":
                    task = st.task
                    if task.n >= 2:
                        dve.wait_ge(full["ou"], gate_tasks[task.n - 2].g2.ou[-1].n + 1)
                    for c, u in enumerate(st.up):
                        dve.wait_ge(full["sc"], u.n + 1)
                        dve.wait_ge(by_act["pp"], st.gate[c].act)
                        dve.tensor_tensor(hgate[:, task.n % 2, c, :], bank("sc", u)[:, :],
                                          silu[:, task.n % 2, c, :], ALU.mult).then_inc(by_dve["sc"], 1)
                        if c == 0:
                            pieces(st, 0, 3)

        @block.tensor
        def _(pe):
            def take(ring, u):
                if u.n >= 2:
                    old = plan.rings[ring][u.n - 2]
                    if old.act is not None:
                        pe.wait_ge(by_act[ring], old.act)
                    if old.dve is not None:
                        pe.wait_ge(by_dve[ring], old.dve)
                return bank(ring, u)

            def turned(stage, group):
                if stage == 0:
                    pe.wait_ge(s_ht[group], 16)
                else:
                    pe.wait_ge(by_act["tr"], plan.turned[GROUPS * (stage - 1) + group].tr[-1].act)

            def product(ps, pairs):
                for i, (lhsT, rhs) in enumerate(pairs):
                    ins = pe.matmul(ps, lhsT, rhs, start=i == 0, stop=i == len(pairs) - 1)
                return ins

            pe.wait_ge(s_const, 5 * 16)
            for st in steps:
                if st.kind == "POS":
                    pe.wait_ge(s_ptab, 16)
                    ps = take("pp", st.pp[0])
                    for k in range(4):
                        pe.wait_ge(s_oh, 4 * st.group + k + 1)
                        ins = pe.matmul(ps[:, :], ptab[:, k, :], onehot[:, (4 * st.group + k) % 2, :],
                                        start=k == 0, stop=k == 3)
                        ins.then_inc(s_ohused if k < 3 else full["pp"], 1)
                if st.kind == "A":
                    task = st.task
                    pe.wait_ge(s_w[task.wset % 2], loaded[task.wset])
                    turned(task.stage, task.group)
                    if task.kind == CROSS0:
                        pe.wait_ge(s_ctx, 16 * KC)
                    if task.kind == CROSS1:
                        pe.wait_ge(s_paired[task.group], 16 * KC)
                    wq, wk, wv, _ = weights(task.kind, task.wset)
                    head = 96 if task.kind == CROSS1 else P
                    for what, i, u, r in st.items:
                        ps = take("pp", u)
                        if what == "q":
                            ins = product(ps[:, :], [(wq[:, c, i * P:(i + 1) * P],
                                                           x_cols(task.stage, c, task.group)) for c in range(KC)])
                        elif what == "k":
                            at = task.group * GT if task.kind == CROSS0 else task.group * 2 * GT + i * GT
                            ins = product(ps[0:head, :], [(wk[:, c, :], HT[:, c, at:at + GT]) for c in range(KC)])
                        else:
                            at = task.group * GT if task.kind == CROSS0 else task.group * 2 * GT + i * GT
                            for n in range(4):
                                ins = product(ps[:, n * head:(n + 1) * head],
                                              [(HT[:, c, at + n * P:at + (n + 1) * P], wv[:, c, :]) for c in range(KC)])
                        ins.then_inc(full["pp"], 1)
                if st.kind == "AQ":
                    task = st.task
                    pe.wait_ge(s_w[task.wset % 2], loaded[task.wset])
                    turned(task.stage, task.group)
                    wq, wk, wv, _ = weights(task.kind, task.wset)
                    at = TOK + task.group * GT + st.part * P
                    ps = take("pp", st.q)
                    for j in range(4):
                        ins = product(ps[:, j * P:(j + 1) * P],
                                      [(wq[:, c, j * P:(j + 1) * P], HT[:, c, at:at + P]) for c in range(KC)])
                    ins.then_inc(full["pp"], 1)
                    ps = take("pp", st.kv)
                    product(ps[:, 0:P], [(wk[:, c, :], HT[:, c, at:at + P]) for c in range(KC)])
                    product(ps[:, P:2 * P], [(HT[:, c, at:at + P], wv[:, c, :])
                                             for c in range(KC)]).then_inc(full["pp"], 1)
                if st.kind == "B":
                    unit = st.unit
                    task = unit.task
                    if task.kind == CROSS1:
                        read(pe, "pp", *task.proj["q"], *task.proj["k"])
                    else:
                        pe.wait_ge(s_rope, unit.rope_done)
                    for i, u in enumerate(st.sc):
                        ps = take("sc", u)
                        if task.kind == HD16:
                            pe.wait_ge(s_kbd, unit.kbd + 1)
                            b = unit.i
                            ins = pe.matmul(ps[:, :], QT[:, b, 2 * i:2 * i + 2, :],
                                            Kbd[:, unit.kbd % 2, :], start=True, stop=True)
                        elif task.kind == CROSS0:
                            for b in range(GB):
                                cols = slice(b * SEQ, (b + 1) * SEQ)
                                ins = pe.matmul(ps[:, cols], QT[:, b, 2 * i:2 * i + 2, :], KT[:, cols],
                                                start=True, stop=True)
                        else:
                            for e in range(2):
                                for h in range(2):
                                    b = 4 * unit.i + 2 * i + e
                                    at = (2 * e + h) * P
                                    ins = pe.matmul(ps[:, at:at + P],
                                                    QT[0:96, b, 2 * h:2 * h + 2, :],
                                                    KT1[0:96, b * P:(b + 1) * P], start=True, stop=True)
                        ins.then_inc(full["sc"], 1)
                if st.kind == "T":
                    unit = st.unit
                    for i, u in enumerate(st.tr):
                        n = 2 * unit.n + i
                        ps = take("tr", u)
                        pe.wait_ge(s_prob, n + 1)
                        for b in range(4):
                            ins = pe.transpose(ps[:, b * P:(b + 1) * P], E[:, n % 4, b * P:(b + 1) * P], ident[:, :])
                        ins.then_inc(full["tr"], 1)
                if st.kind == "C":
                    unit = st.unit
                    task = unit.task
                    pe.wait_ge(by_act["tr"], unit.t.tr[1].act)
                    read(pe, "pp", *task.proj["v"])
                    v = v_buf(task)
                    pt = PT[:, unit.n % 2, :]
                    if task.kind == CROSS0:
                        ps = [take("ou", u) for u in st.ou]
                        for x in range(2):
                            for e in range(2):
                                i = 2 * st.part + x
                                rows = slice(64 * e, 64 * e + 64)
                                ins = pe.matmul(ps[e][:, x * 256:(x + 1) * 256], v[rows, i * P:(i + 1) * P],
                                                pt[rows, i * 256:(i + 1) * 256], start=True, stop=True)
                                if x:
                                    ins.then_inc(full["ou"], 1)
                        continue
                    for i, u in enumerate(st.ou):
                        ps = take("ou", u)
                        if task.kind == HD16:
                            pe.wait_ge(s_vbd, unit.kbd + 1)
                            ins = product(ps[:, 0:256], [(VB[:, unit.kbd % 2, g * P:(g + 1) * P],
                                                          pt[:, g * 256:(g + 1) * 256]) for g in range(4)])
                        else:
                            for e in range(2):
                                b = 4 * unit.i + 2 * i + e
                                at = (2 * i + e) * 256
                                ins = pe.matmul(ps[0:96, e * 256:(e + 1) * 256], v[:, b * 96:(b + 1) * 96],
                                                pt[:, at:at + 256], start=True, stop=True)
                        ins.then_inc(full["ou"], 1)
                if st.kind == "D":
                    task = st.task
                    wo = weights(task.kind, task.wset)[3]
                    if task.wset == 0:
                        pe.wait_ge(s_first_o, 16)
                    pe.wait_ge(by_act["ou"], st.needs.act)
                    for i, u in zip(st.tiles, st.ou):
                        ps = take("ou", u)
                        product(ps[:, :], [(OT[:, j, i * P:(i + 1) * P], wo[:, j, :])
                                           for j in range(3 if task.kind == CROSS1 else 4)]).then_inc(full["ou"], 1)
                if st.kind == "LNT":
                    for i, u in enumerate(st.tr):
                        ps = take("tr", u)
                        pe.wait_ge(s_xn, TILES * st.n + i + 1)
                        for c in range(KC):
                            ins = pe.transpose(ps[:, c * P:(c + 1) * P],
                                               X[:, st.group * TILES + i, c * P:(c + 1) * P], ident[:, :])
                        ins.then_inc(full["tr"], 1)
                if st.kind == "Z":
                    pe.wait_ge(s_fc, 48)
                    pe.wait_ge(s_fcb, 2)
                    turned(2, st.group)
                    ps = take("pp", st.pp[0])
                    product(ps[0:RANK, :], [(c1_sb[:, c, :], x_cols(2, c, st.group))
                                            for c in range(KC)]).then_inc(full["pp"], 1)
                if st.kind == "F1":
                    task = st.task
                    sub = task.sub
                    w1, _ = ffn_weights(wslot(task.wset))
                    if sub == 0:
                        z = next(s for s in steps if s.kind == "Z" and s.group == task.group)
                        read(pe, "pp", z.pp[0])

                    def first_products(c):
                        pe.wait_ge(s_w[task.wset % 2], loaded[task.wset])
                        ps = take("pp", st.pp[c])
                        product(ps[:, :], [(w1[:, k, c * P:(c + 1) * P], x_cols(2, k, task.group))
                                           for k in range(KC)]).then_inc(full["pp"], 1)

                    first_products(0)
                    for i2, u in enumerate(st.sc):
                        ps = take("sc", u)
                        for e in range(2):
                            at = task.group * GT + (2 * i2 + e) * P
                            ins = pe.matmul(ps[:, e * ROW:(e + 1) * ROW], zT[:, at:at + P],
                                            c2_sb[:, sub * ROW:(sub + 1) * ROW], start=True, stop=True)
                        ins.then_inc(full["sc"], 1)
                    first_products(1)
                if st.kind == "F2":
                    task = st.task
                    pe.wait_ge(by_dve["sc"], task.f1.sc[1].dve)
                    for c, u in enumerate(st.tr):
                        ps = take("tr", u)[:, 0:256].bitcast(BF16)
                        for i in range(TILES):
                            ins = pe.transpose(ps[:, i * P:(i + 1) * P], chosen[:, task.n % 2, i, c * P:(c + 1) * P],
                                               ident_b)
                        ins.then_inc(full["tr"], 1)
                if st.kind == "F3":
                    task = st.task
                    for c, u in enumerate(st.sc):
                        ps = take("sc", u)
                        pe.wait_ge(by_act["tr"], task.f2.tr[c].act)
                        pe.matmul(ps[:, :], ties, chosenT[:, c, :], start=True, stop=True).then_inc(full["sc"], 1)
                if st.kind == "F4":
                    task = st.task
                    _, w2 = ffn_weights(wslot(task.wset))
                    pe.wait_ge(by_dve["sc"], task.f3.sc[1].dve)
                    for i, u in enumerate(st.ou):
                        ps = take("ou", u)
                        product(ps[:, :], [(hsel[:, c, i * P:(i + 1) * P], w2[:, c, :])
                                           for c in range(2)]).then_inc(full["ou"], 1)
                if st.kind == "G1":
                    task = st.task
                    if task.sub == 0:
                        turned(5, task.group)
                    pe.wait_ge(s_dqd, 3 * task.sub + 2)
                    mats = [dq[task.sub % 3][:, 1024 * m:1024 * m + 1024].rearrange("p (c n) -> p c n", c=KC)
                            for m in range(2)]
                    for c in range(2):
                        for ring, u, w in (("pp", st.gate[c], mats[0]), ("sc", st.up[c], mats[1])):
                            ps = take(ring, u)
                            product(ps[:, :], [(w[:, k, c * P:(c + 1) * P], x_cols(5, k, task.group))
                                               for k in range(KC)]).then_inc(full[ring], 1)
                if st.kind == "G2":
                    task = st.task
                    pe.wait_ge(s_dqd, 3 * task.sub + 3)
                    pe.wait_ge(by_dve["sc"], task.g1.up[1].dve)
                    w = dq[task.sub % 3][:, 2048:3072].rearrange("p (c n) -> p c n", c=2)
                    for i, u in enumerate(st.ou):
                        ps = take("ou", u)
                        product(ps[:, :], [(hgate[:, task.n % 2, c, i * P:(i + 1) * P], w[:, c, :])
                                           for c in range(2)]).then_inc(full["ou"], 1)


def constants():
    p = np.arange(P)
    c = {"ident": np.eye(P, dtype=np.float32)}
    c["causal"] = np.where(np.arange(SEQ)[None, :] > (p % SEQ)[:, None], np.float32(FUTURE), np.float32(0))
    c["own_head"] = (((p % 64) // 8)[:, None] == np.arange(8)[None, :]).astype(np.float32)
    c["iota"] = (p[:, None] + P * np.arange(4)[None, :]).astype(np.float32)

    def tables(length, dim):
        inv = (1.0 / np.float32(10000.0) ** (np.arange(0, dim, 2, dtype=np.float32) / np.float32(dim))).astype(np.float32)
        ang = np.outer(np.arange(length, dtype=np.float32), inv).astype(np.float32)
        return np.cos(ang).astype(np.float32), np.sin(ang).astype(np.float32)

    cos, sin = tables(SEQ, 16)
    sign = np.where(p < 64, -1, 1).astype(np.float32)
    c["rope16"] = np.stack([cos.T[p % 8], sin.T[p % 8] * sign[:, None]], 1).astype(np.float32)
    cos, sin = tables(POSITIONS, P)
    c["ptab"] = np.concatenate([cos, sin], 1).astype(np.float32)
    same = (p[:, None] // BLK) == (p[None, :] // BLK)
    c["ties"] = ((same & (p[:, None] < p[None, :])).astype(np.float32)
                 - np.float32(TIE) * np.eye(P, dtype=np.float32)).astype(np.float32)
    return c


def kernel(**inputs):
    import concourse.bacc as _bacc
    from concourse.bass_utils import run_bass_kernel_spmd as _run

    a = {k: np.asarray(v) for k, v in inputs.items()}
    arrays = {}

    def lay(name, value):
        arrays[name] = np.ascontiguousarray(value)

    lay("x_tok", a["x"].reshape(TOK, DIM))
    lay("x_T", a["x"].reshape(TOK, DIM).T)
    lay("ctx_T", a["ctx_4096"].reshape(TOK, DIM).T)
    lay("pos", a["pos_BxS2"].reshape(1, TOK))
    lay("mask", a["mask_BxSxS2_ik0"])

    def by_half(w, heads):
        w = w.reshape(DIM, 8, heads // 8, 2, 8)
        return w.transpose(0, 2, 3, 1, 4).reshape(DIM, heads * 16)

    def out_rows(w):
        return w.reshape(8, 4, 16, DIM).transpose(1, 0, 2, 3).reshape(DIM, DIM)

    def packed(w):
        w = w.reshape(DIM, 4, 4, 96)
        return np.concatenate([w[:, :, 0:3, :], w[:, :, 3, :].reshape(DIM, 4, 3, 32)], 3).reshape(DIM, 1536)

    for layer, turn in ((0, True), (1, False)):
        w = {n: a[f"L{layer}_attn_W{n}"] for n in "qkvo"}
        if turn:
            w = {n: v.T for n, v in w.items()}
        lay(f"hd{layer}_q", by_half(w["q"], 32))
        lay(f"hd{layer}_k", by_half(w["k"], 8))
        lay(f"hd{layer}_v", w["v"])
        lay(f"hd{layer}_o", out_rows(w["o"]))
    for n in "qkvo":
        lay(f"cross0_{n}", a[f"L0_xattn_W{n}"])
        w = a[f"L1_xattn_W{n}"].T
        lay(f"cross1_{n}", packed(w) if n == "q" else packed(w.T).T if n == "o" else w)
    lay("c1T", a["L0_ffn_c1_w"].T)
    lay("c2T", a["L0_ffn_c2_w"].T)
    lay("w1T", a["L0_ffn_w1"].T)
    lay("w2t", a["L0_ffn_w2t"])
    lay("gate_q", a["L1_ffn_gate_q"].T)
    lay("up_q", a["L1_ffn_up_q"].T)
    lay("down_q", a["L1_ffn_down_q"].T)
    lay("gate_s", a["L1_ffn_gate_absmax"].reshape(INTER, DIM // 64).T)
    lay("up_s", a["L1_ffn_up_absmax"].reshape(INTER, DIM // 64).T)
    lay("down_s", a["L1_ffn_down_absmax"].reshape(DIM, INTER // 64).T)
    consts = constants()
    for n, v in consts.items():
        lay(f"const_{n}", v)

    nc = _bacc.Bacc("TRN2", target_bir_lowering=False, num_devices=1)
    d = {n: nc.dram_tensor(n, v.shape, mybir.dt.from_np(v.dtype), kind="ExternalInput").ap() for n, v in arrays.items()}
    out = nc.dram_tensor("out", (TOK, DIM), F32, kind="ExternalOutput").ap()
    decoder_kernel(nc, d["x_tok"], d["x_T"], d["ctx_T"], d["pos"], d["mask"],
                   [[d[f"hd{i}_{n}"] for n in "qkvo"] for i in range(2)],
                   [d[f"cross0_{n}"] for n in "qkvo"],
                   d["c1T"], d["c2T"], d["w1T"], d["w2t"],
                   [d[f"cross1_{n}"] for n in "qkvo"],
                   d["gate_q"], d["gate_s"], d["up_q"], d["up_s"], d["down_q"], d["down_s"],
                   {n: d[f"const_{n}"] for n in consts}, out)
    r = _run(nc, [arrays], core_ids=[0])
    return r.results[0]["out"].reshape(BATCH, SEQ, DIM)
```
